# Optimizing a Trainium2 kernel written in Bass

```python
import numpy as np
import jax
import jax.numpy as jnp

def _softmax(x, axis=-1):
    return jax.nn.softmax(x, axis=axis)

def _gelu(x):
    return jax.nn.gelu(x, approximate=True)

def _silu(x):
    return jax.nn.silu(x)

def _sigmoid(x):
    return jax.nn.sigmoid(x)

def _layernorm(x, axis=-1, eps=1e-05):
    m = jnp.mean(x, axis=axis, keepdims=True)
    v = jnp.var(x, axis=axis, keepdims=True)
    return (x - m) / jnp.sqrt(v + eps)

def _scatter_add(tgt, idx, src, axis=0):
    return tgt.at[idx].add(src)

def _segment_sum(src, seg, n):
    return jax.ops.segment_sum(src, seg, n)
kernel_name = 'mk_adaln_ffn_d2_seqx_r8_608274'

def setup_inputs(seed: int=0):
    np.random.seed(seed)
    _w = jnp.asarray

    def _rec_inputs():
        import jax
        import jax.numpy as jnp
        _rk = jax.random.key(seed)
        x = -0.000125 + 0.9999 * jax.random.normal(jax.random.fold_in(_rk, 1), (64, 32, 512), jnp.float32)
        _lenS = 32 - jax.random.randint(jax.random.fold_in(_rk, 7), (64,), 0, max(1, 32 // 4) + 1, jnp.int32)
        _lenS2 = 32 - jax.random.randint(jax.random.fold_in(_rk, 8), (64,), 0, max(1, 32 // 4) + 1, jnp.int32)
        cond_128 = 0.0061147 + 1.02565 * jax.random.normal(jax.random.fold_in(_rk, 11), (64, 128), jnp.float32)
        fside_S_0 = -0.022604 + 0.987366 * jax.random.normal(jax.random.fold_in(_rk, 12), (32,), jnp.float32)
        return (x, cond_128, fside_S_0)
    x, cond_128, fside_S_0 = _rec_inputs()

    def _L0_cond_setup():
        import jax, jax.numpy as jnp
        import numpy as np
        K = 8
        T = 1.0
        D_EMBD = 128
        IN_C = 32
        OUT_C = 32
        BS = 32
        H = 512
        HID = 128
        key = jax.random.key(seed)
        ks = jax.random.split(key, 10)
        s = lambda fan_in: 1.0 / np.sqrt(fan_in)
        return {'x': jax.random.normal(ks[0], (BS, IN_C, H), dtype=jnp.float32), 'embedding': jax.random.normal(ks[1], (BS, D_EMBD), dtype=jnp.float32), 'W0': jax.random.normal(ks[2], (D_EMBD, HID), dtype=jnp.float32) * s(D_EMBD), 'b0': jnp.zeros((HID,), dtype=jnp.float32), 'W1': jax.random.normal(ks[3], (HID, HID), dtype=jnp.float32) * s(HID), 'b1': jnp.zeros((HID,), dtype=jnp.float32), 'W2': jax.random.normal(ks[4], (HID, K), dtype=jnp.float32) * s(HID), 'b2': jnp.zeros((K,), dtype=jnp.float32), 'weight': jax.random.normal(ks[5], (K, OUT_C, IN_C, 1), dtype=jnp.float32) * s(IN_C), 'bias_k': jax.random.normal(ks[6], (K, OUT_C), dtype=jnp.float32) * 0.1}
    _L0_cond_all = _L0_cond_setup()
    _L0_cond_in = {k: v for k, v in _L0_cond_all.items() if k in ('W0', 'b0', 'W1', 'b1', 'W2', 'b2', 'weight', 'bias_k')}
    del _L0_cond_all

    def _L0_ffn_setup():
        import jax, jax.numpy as jnp
        import numpy as np
        import math
        B, S, IN, OUT = (4, 256, 512, 512)
        E, R, K = (8, 64, 128)
        SCALE = 64.0 / 64.0
        MULTIPLIER = 1.0
        key = jax.random.key(seed)
        ks = jax.random.split(key, 6)
        return {'x': jax.random.normal(ks[0], (B, S, IN), jnp.float32), 'W_org': jax.random.normal(ks[1], (OUT, IN), jnp.float32) * 0.02, 'lora_down': jax.random.normal(ks[2], (E, IN, R), jnp.float32) * 0.02, 'lora_up': jax.random.normal(ks[3], (E, R, OUT), jnp.float32) * 0.02, 'lora_keys': jax.random.normal(ks[4], (E, K), jnp.float32), 'Wq': jax.random.normal(ks[5], (K, IN), jnp.float32) * 0.02}
    _L0_ffn_all = _L0_ffn_setup()
    _L0_ffn_in = {k: v for k, v in _L0_ffn_all.items() if k in ('W_org', 'lora_down', 'lora_up', 'lora_keys', 'Wq')}
    del _L0_ffn_all

    def _L1_cond_setup():
        import jax, jax.numpy as jnp
        import numpy as np
        from jax import lax
        N, C_IN, L = (32, 32, 512)
        C_OUT, K, GROUPS = (32, 9, 4)
        C_DIM, PAD, STRIDE = (128, 4, 1)
        key = jax.random.key(seed)
        k1, k2, k3, k4, k5 = jax.random.split(key, 5)
        x = jax.random.normal(k1, (N, C_IN, L), dtype=jnp.float32)
        c = jax.random.normal(k2, (N, C_DIM), dtype=jnp.float32)
        weight = jax.random.normal(k3, (C_OUT, C_IN // GROUPS, K), dtype=jnp.float32)
        c_weight = jax.random.normal(k4, (C_OUT, C_DIM), dtype=jnp.float32)
        bias = jax.random.normal(k5, (C_OUT,), dtype=jnp.float32)
        return {'x': x, 'c': c, 'weight': weight, 'c_weight': c_weight, 'bias': bias}
    _L1_cond_all = _L1_cond_setup()
    _L1_cond_in = {k: v for k, v in _L1_cond_all.items() if k in ('weight', 'c_weight')}
    del _L1_cond_all

    def _L1_ffn_setup():
        import jax, jax.numpy as jnp
        import numpy as np
        B, L, H, Dh, M = (4, 256, 16, 32, 128)
        D = H * Dh
        key = jax.random.key(seed)
        kx, ku, kd, kp = jax.random.split(key, 4)
        x = jax.random.normal(kx, (B, L, D), dtype=jnp.float32)
        up = jax.random.normal(ku, (H, Dh, M), dtype=jnp.float32)
        down = jax.random.normal(kd, (H, M, Dh), dtype=jnp.float32)
        perm = jax.random.permutation(kp, D)
        return {'x': x, 'up': up, 'down': down, 'perm': perm}
    _L1_ffn_all = _L1_ffn_setup()
    _L1_ffn_in = {k: v for k, v in _L1_ffn_all.items() if k in ('up', 'down', 'perm')}
    del _L1_ffn_all
    return {'x': x, 'cond_128': cond_128, 'fside_S_0': fside_S_0, 'L0_cond_W0': _L0_cond_in['W0'], 'L0_cond_b0': _L0_cond_in['b0'], 'L0_cond_W1': _L0_cond_in['W1'], 'L0_cond_b1': _L0_cond_in['b1'], 'L0_cond_W2': _L0_cond_in['W2'], 'L0_cond_b2': _L0_cond_in['b2'], 'L0_cond_weight': _L0_cond_in['weight'], 'L0_cond_bias_k': _L0_cond_in['bias_k'], 'L0_ffn_W_org': _L0_ffn_in['W_org'], 'L0_ffn_lora_down': _L0_ffn_in['lora_down'], 'L0_ffn_lora_up': _L0_ffn_in['lora_up'], 'L0_ffn_lora_keys': _L0_ffn_in['lora_keys'], 'L0_ffn_Wq': _L0_ffn_in['Wq'], 'L1_cond_weight': _L1_cond_in['weight'], 'L1_cond_c_weight': _L1_cond_in['c_weight'], 'L1_ffn_up': _L1_ffn_in['up'], 'L1_ffn_down': _L1_ffn_in['down'], 'L1_ffn_perm': _L1_ffn_in['perm']}

def reference(x, cond_128, fside_S_0, L0_cond_W0, L0_cond_b0, L0_cond_W1, L0_cond_b1, L0_cond_W2, L0_cond_b2, L0_cond_weight, L0_cond_bias_k, L0_ffn_W_org, L0_ffn_lora_down, L0_ffn_lora_up, L0_ffn_lora_keys, L0_ffn_Wq, L1_cond_weight, L1_cond_c_weight, L1_ffn_up, L1_ffn_down, L1_ffn_perm):
    import jax
    import jax.numpy as jnp

    def _L0_cond_ref(x, embedding, W0, b0, W1, b1, W2, b2, weight, bias_k):
        import jax, jax.numpy as jnp
        import numpy as np
        K = 8
        T = 1.0
        D_EMBD = 128
        IN_C = 32
        OUT_C = 32
        BS = 32
        H = 512
        HID = 128
        h = jax.nn.gelu(embedding @ W0 + b0, approximate=False)
        h = jax.nn.gelu(h @ W1 + b1, approximate=False)
        att = jax.nn.softmax((h @ W2 + b2) / T, axis=-1)
        agg_w = jnp.einsum('bk,koi->boi', att, weight[..., 0])
        agg_b = att @ bias_k
        out = jnp.einsum('boi,bih->boh', agg_w, x) + agg_b[:, :, None]
        return out

    def _L0_ffn_ref(x, W_org, lora_down, lora_up, lora_keys, Wq):
        import jax, jax.numpy as jnp
        import numpy as np
        import math
        B, S, IN, OUT = (4, 256, 512, 512)
        E, R, K = (8, 64, 128)
        SCALE = 64.0 / 64.0
        MULTIPLIER = 1.0
        base = jnp.einsum('bsi,oi->bso', x, W_org)
        q = jnp.einsum('bi,ki->bk', x.mean(axis=1), Wq)
        scores = jnp.einsum('bk,ek->be', q, lora_keys) / math.sqrt(K)
        coeffs = jax.nn.softmax(scores, axis=-1)
        h = jnp.einsum('bsi,eir->bser', x, lora_down)
        delta = jnp.einsum('be,bser,ero->bso', coeffs, h, lora_up)
        return base + delta * (SCALE * MULTIPLIER)

    def _L1_cond_ref(x, c, weight, c_weight, bias):
        import jax, jax.numpy as jnp
        import numpy as np
        from jax import lax
        N, C_IN, L = (32, 32, 512)
        C_OUT, K, GROUPS = (32, 9, 4)
        C_DIM, PAD, STRIDE = (128, 4, 1)
        out = lax.conv_general_dilated(x, weight, window_strides=(STRIDE,), padding=[(PAD, PAD)], dimension_numbers=('NCH', 'OIH', 'NCH'), feature_group_count=GROUPS)
        ctx = jnp.einsum('nd,od->no', c, c_weight)
        out = out + ctx[:, :, None] + bias[None, :, None]
        return out

    def _L1_ffn_ref(x, up, down, perm):
        import jax, jax.numpy as jnp
        import numpy as np
        B, L, H, Dh, M = (4, 256, 16, 32, 128)
        D = H * Dh
        b, l, Dm = x.shape
        h, d = (up.shape[0], up.shape[1])
        unperm = jnp.argsort(perm)
        t = x.reshape(b * l, Dm)
        t = t[:, perm]
        t = t.reshape(b * l, h, d)
        t = jnp.einsum('bhd,hdm->bhm', t, up)
        t = jax.nn.gelu(t, approximate=False)
        t = jnp.einsum('bhm,hmd->bhd', t, down)
        t = t.reshape(b * l, h * d)
        t = t[:, unperm]
        out = t.reshape(b, l, Dm)
        return out
    x = x + _L0_ffn_ref(_L0_cond_ref(x, cond_128, L0_cond_W0, L0_cond_b0, L0_cond_W1, L0_cond_b1, L0_cond_W2, L0_cond_b2, L0_cond_weight, L0_cond_bias_k), L0_ffn_W_org, L0_ffn_lora_down, L0_ffn_lora_up, L0_ffn_lora_keys, L0_ffn_Wq)
    x = x + _L1_ffn_ref(_L1_cond_ref(x, cond_128, L1_cond_weight, L1_cond_c_weight, fside_S_0), L1_ffn_up, L1_ffn_down, L1_ffn_perm)
    return x

_drawn_inputs = setup_inputs


def setup_inputs(seed=0):
    import zlib

    import numpy as np

    out = dict(_drawn_inputs(seed))
    spreads = {'L0_cond_b0': (0.0, 0.8), 'L0_cond_b1': (0.0, 0.8), 'L0_cond_b2': (0.0, 0.8)}
    factors = {'L0_cond_bias_k': 6.231,
     'L0_ffn_lora_down': 8.0,
     'L0_ffn_lora_up': 8.0,
     'L0_ffn_lora_keys': 8.0,
     'L0_ffn_Wq': 8.0}
    for name, (base, spread) in spreads.items():
        noise = np.random.default_rng([zlib.crc32(name.encode()), seed]).standard_normal(out[name].shape)
        drawn = base * np.exp(spread * noise) if base else spread * noise
        out[name] = jnp.asarray(drawn.astype(out[name].dtype))
    for name, factor in factors.items():
        out[name] = (out[name] * factor).astype(out[name].dtype)
    return out
```

```python
from contextlib import ExitStack

import numpy as np

import concourse.bass as bass
from concourse import mybir

ALU = mybir.AluOpType
ACT = mybir.ActivationFunctionType
AX = mybir.AxisListType
F32 = mybir.dt.float32
F32R = mybir.dt.float32r
I32 = mybir.dt.int32

P = 128
B, C, L = 64, 32, 512
E, R, KD = 8, 64, 128
NK = 8
H, DH, MH = 16, 32, 128
TAPS, CG = 9, 8
PH = 4
M = L // PH
BG = P // C
NG = 2
NCH = B // (BG * NG)
TN = P * NG
CB = BG * NG
BANK = 512
TPB = BANK // TN
NL = (E * R // P) // TPB
HPB = BANK // TN
NB = H // HPB
HT = H * DH // P
HPT = P // DH
GR = 8
KR = GR // HPB
SCORE_SCALE = 1.0 / (C * float(KD) ** 0.5)
assert NG == 2 and NL == 2
TAPB = 3

PACK_A = dict(condT=B, W0=P, W1=P, W2=NK, b0=1, b1=1, ident=P)
PACK_B = dict(keysT=E, cwT=C, side=C, Wq=L, W3=TAPB * P, dn=H * DH)


def offsets(pack):
    at, out = 0, {}
    for name, n in pack.items():
        out[name] = (at, at + n)
        at += n
    return out, at


def adaln_ffn(nc, x, pack_a, pack_b, wK, bk, b2, Wt, down, up, upf, idx_gather, idx_scatter, out):
    col_a, width_a = offsets(PACK_A)
    col_b, width_b = offsets(PACK_B)
    ctx = ExitStack()
    with ctx:
        def sb(name, shape, dt=F32):
            return ctx.enter_context(nc.sbuf_tensor(name, shape, dt))

        def sem(name):
            return ctx.enter_context(nc.semaphore(name))

        def bank(name):
            return ctx.enter_context(nc.psum_tensor(name, [P, BANK], F32))

        ps_a = [bank("ps_a0"), bank("ps_a1")]
        ps_b = [bank("ps_b0"), bank("ps_b1")]
        ps_up = [bank("ps_up0"), bank("ps_up1")]
        ps_dn = bank("ps_dn")
        ps_c = bank("ps_c")

        pa = sb("pa", [P, width_a])
        pb = sb("pb", [P, width_b])

        def A(name):
            return pa[:, col_a[name][0]:col_a[name][1]]

        def Bp(name):
            return pb[:, col_b[name][0]:col_b[name][1]]

        wK_sb = sb("wK_sb", [NK, C, P])
        bk_sb = sb("bk_sb", [NK, C])
        b2_sb = sb("b2_sb", [B, NK])
        ones = sb("ones", [P, P])
        stage_w = sb("stage_w", [P, 2, PH * L])
        stage_o = sb("stage_o", [P, B * C])
        Wt_h, Wt_l = sb("Wt_h", [P, PH, L], F32R), sb("Wt_l", [P, PH, L], F32R)
        dw_h, dw_l = sb("dw_h", [P, PH, L], F32R), sb("dw_l", [P, PH, L], F32R)
        up_h, up_l = sb("up_h", [P, PH, L], F32R), sb("up_l", [P, PH, L], F32R)
        upf_s = sb("upf_s", [P, H, MH], F32R)
        mixer = sb("mixer", [P, B // BG, P])
        mix_bias = sb("mix_bias", [P, B * C])
        conv_bias = sb("conv_bias", [P, B * C])
        route = sb("route", [P, PH, E])
        h1, h2 = sb("h1", [P, B]), sb("h2", [P, B])
        lg, att = sb("lg", [B, NK]), sb("att", [B, NK])
        attT = sb("attT", [NK, B])
        stat = sb("stat", [B, 4])
        ig = sb("ig", [P, H], I32)
        isc = sb("isc", [P, HT], I32)

        xs = sb("xs", [P, NG, L])
        yf = sb("yf", [P, 2, L])
        y_h, y_l = sb("y_h", [P, PH, TN], F32R), sb("y_l", [P, PH, TN], F32R)
        ysum = sb("ysum", [P, PH, CB])
        sc_st = sb("sc_st", [CB, 4])
        coef_e = sb("coef_e", [CB, E])
        coef = sb("coef", [CB, E])
        coef_b = sb("coef_b", [CB, E, R])
        coefT = sb("coefT", [P, PH, CB])
        hf = sb("hf", [P, 2, TPB, TN])
        h_h, h_l = sb("h_h", [P, PH, TN], F32R), sb("h_l", [P, PH, TN], F32R)
        x1 = sb("x1", [P, NG, L])
        x1p = sb("x1p", [P, CB, M + 2])
        zf = sb("zf", [P, 2, BANK])
        z_h, z_l = sb("z_h", [P, PH, TN], F32R), sb("z_l", [P, PH, TN], F32R)
        x1T = sb("x1T", [P, PH, TN])
        gat = sb("gat", [P, GR, TN], F32R)
        act = sb("act", [P, KR, BANK])
        oT = sb("oT", [P, 2, TN])

        ztab = nc.dram_tensor("ztab", (2 * L, TN), F32, kind="Internal").ap()

        s_pa, s_pb, s_wk, s_idx = sem("pack_a_in"), sem("pack_b_in"), sem("kernels_in"), sem("index_in")
        s_wd, s_ww, s_wu, s_wf = sem("down_in"), sem("worg_in"), sem("up_in"), sem("heads_up_in")
        s_one = sem("ones_set")
        s_mz = sem("mixer_zeroed")
        s_pz = sem("pads_zeroed")
        s_cp = sem("cond_product")
        s_cg = sem("cond_gelu")
        s_dv = sem("vector_setup")
        s_ce = sem("cond_exp")
        s_mk = sem("mixer_product")
        s_mc = sem("mixer_copied")
        s_bp = sem("bias_product")
        s_mb = sem("mix_bias_set")
        s_cb = sem("conv_bias_set")
        s_rp, s_rt = sem("route_product"), sem("route_set")
        s_hw, s_lw = sem("weights_high"), sem("weights_low")
        s_x = [sem(f"x_in{g}") for g in range(NG)]
        s_mix, s_yf, s_yh, s_yl, s_ys = sem("mixed"), sem("y_full"), sem("y_high"), sem("y_low"), sem("y_summed")
        s_sc, s_sm, s_se, s_sr = sem("scores"), sem("scores_max"), sem("scores_exp"), sem("scores_recip")
        s_cf, s_ct, s_cc = sem("coef_ready"), sem("coef_turned"), sem("coefT_copied")
        s_lo, s_hf, s_hh, s_hl = sem("lora_down"), sem("h_full"), sem("h_high"), sem("h_low")
        s_bu, s_x1 = sem("base_and_up"), sem("x1_ready")
        s_xp = [sem(f"x1_phases{g}") for g in range(NG)]
        s_cv, s_zf, s_zh, s_zl = sem("convolved"), sem("z_full"), sem("z_high"), sem("z_low")
        s_xt, s_xe = sem("x1_turned"), sem("x1T_copied")
        s_xo = [sem(f"x1T_out{g}") for g in range(NG)]
        s_zt = [sem(f"z_table{g}") for g in range(NG)]
        s_g = [sem(f"gathered{s}") for s in range(GR)]
        s_up, s_ga, s_dn, s_oe = sem("heads_up"), sem("activated"), sem("heads_down"), sem("oT_copied")
        s_so = [sem(f"scattered{s}") for s in range(2)]
        s_ix = sem("index_stepped")

        def before(eng, s, value):
            if not isinstance(value, int) or value > 0:
                eng.wait_ge(s, value)

        block = ctx.enter_context(nc.Block())

        @block.sync
        def _(sp):
            def load_x(i, g):
                before(sp, s_x1, NG * (i - 1) + g + 1)
                sp.dma_start(xs[:, g, :], x[bass.ds((i * NG + g) * P, P), :]).then_inc(s_x[g], 16)

            def phases(i, g):
                sp.wait_ge(s_x1, NG * i + g + 1)
                before(sp, s_xt, NG * (i - 1) + g + 1)
                for b in range(BG):
                    sp.dma_start(x1p[:, BG * g + b, 1:1 + M],
                                 x1[C * b:C * b + C, g, :].rearrange("c (r m) -> c r m", r=PH)).then_inc(s_xp[g], 16)

            def store_z(j, g):
                if g == 0:
                    for s in range(GR):
                        before(sp, s_g[s], 16 * (H // GR) * j)
                cols = slice(P * g, P * g + P)
                sp.wait_ge(s_zh, NG * j + g + 1)
                sp.dma_start(ztab[0:L, cols].rearrange("(m r) t -> m r t", r=PH),
                             z_h[:, :, cols].bitcast(F32)).then_inc(s_zt[g], 16)
                sp.wait_ge(s_zl, NG * j + g + 1)
                sp.dma_start(ztab[L:2 * L, cols].rearrange("(m r) t -> m r t", r=PH),
                             z_l[:, :, cols].bitcast(F32)).then_inc(s_zt[g], 16)
                sp.wait_ge(s_xe, NG * j + g + 1)
                sp.dma_start(out[:, bass.ds(j * TN + P * g, P)].rearrange("(m r) t -> m r t", r=PH),
                             x1T[:, :, cols]).then_inc(s_xo[g], 16)

            def chunk(i, more=True):
                if not isinstance(i, int) or i > 0:
                    for g in range(NG):
                        store_z(i - 1, g)
                for g in range(NG):
                    phases(i, g)
                    if more:
                        load_x(i + 1, g)

            sp.dma_start(pa[:, :], pack_a).then_inc(s_pa, 16)
            sp.dma_start(wK_sb[:, :, :], wK).then_inc(s_wk, 16)
            for g in range(NG):
                load_x(0, g)
            sp.dma_start(stage_w[:, 0, :], down).then_inc(s_wd, 16)
            sp.dma_start(stage_w[:, 1, :], Wt).then_inc(s_ww, 16)
            sp.dma_start(pb[:, :], pack_b).then_inc(s_pb, 16)
            sp.wait_ge(s_lw, 1)
            sp.dma_start(stage_w[:, 0, :], up).then_inc(s_wu, 16)
            sp.wait_ge(s_lw, 2)
            for q in range(HPT):
                sp.dma_start(stage_w[DH * q:DH * q + DH, 1, :], upf).then_inc(s_wf, 16)
            sp.wait_ge(s_pz, 1)
            chunk(0)
            chunk(1)
            with sp.Fori(2, NCH - 1) as i:
                chunk(i)
            chunk(NCH - 1, more=False)
            for g in range(NG):
                store_z(NCH - 1, g)
            for g in range(NG):
                sp.wait_ge(s_xo[g], 16 * NCH)
            for s in range(2):
                sp.wait_ge(s_so[s], 16 * (HT // 2) * NCH)

        @block.gpsimd
        def _(pool):
            limit = pool.alloc_register("limit")

            def value(v):
                if isinstance(v, int):
                    return v
                pool.reg_mov(limit, v)
                return limit

            def gather(j, h):
                free = value(NB * j + (h - GR) // HPB + 1 if h >= GR else NB * (j - 1) + (h + H - GR) // HPB + 1)
                pool.wait_ge(s_ix, 3)
                before(pool, s_up, free)
                pool.indirect_dma_start(
                    out=gat[:, h % GR, :].bitcast(F32), out_offset=None, in_=ztab,
                    in_offset=bass.IndirectOffsetOnAxis(ap=ig[:, h:h + 1], axis=0),
                ).then_inc(s_g[h % GR], 16)

            def scatter(j, t):
                ready = value(HT * j + t + 1)
                pool.wait_ge(s_ix, 3)
                pool.wait_ge(s_oe, ready)
                pool.indirect_dma_start(
                    out=out.rearrange("l (c t) -> (l c) t", t=TN),
                    out_offset=bass.IndirectOffsetOnAxis(ap=isc[:, t:t + 1], axis=0),
                    in_=oT[:, t % 2, :], in_offset=None, compute_op=ALU.add,
                ).then_inc(s_so[t % 2], 16)

            def chunk(j):
                for g in range(NG):
                    pool.wait_ge(s_zt[g], 32 * (j + 1))
                for h in range(GR + HPT):
                    gather(j, h)
                if not isinstance(j, int) or j > 0:
                    done = value(16 * (HT // 2) * j)
                    pool.wait_ge(s_ix, 3)
                    for s in range(2):
                        pool.wait_ge(s_so[s], done)
                    pool.tensor_scalar(isc[:, :], isc[:, :], 1.0, None, ALU.add).then_inc(s_ix, 1)
                    pool.wait_ge(s_ix, j + 3)
                for g in range(NG):
                    pool.wait_ge(s_xo[g], 16 * (j + 1))
                scatter(j, 0)
                for h in range(GR + HPT, H):
                    gather(j, h)
                for t in range(1, HT):
                    scatter(j, t)

            pool.memset(mixer[:, :, :], 0.0).then_inc(s_mz, 1)
            pool.memset(x1p[:, :, :], 0.0).then_inc(s_pz, 1)
            pool.wait_ge(s_idx, 32)
            pool.wait_ge(s_mz, 1)
            pool.wait_ge(s_pz, 1)
            for n, q in enumerate((1, 3)):
                rows = slice(DH * q, DH * q + DH)
                pool.tensor_scalar(ig[rows, :], ig[rows, :], float(L), None, ALU.add).then_inc(s_ix, 1)
                pool.wait_ge(s_ix, n + 1)
            pool.tensor_scalar(isc[:, :], isc[:, :], float(NCH), None, ALU.mult).then_inc(s_ix, 1)
            pool.wait_ge(s_ix, 3)
            chunk(0)
            with pool.Fori(1, NCH) as j:
                chunk(j)

        @block.scalar
        def _(sc):
            def high(dst, src, s, value):
                sc.wait_ge(s, value)
                sc.copy(dst, src).then_inc(s_hw, 1)

            def y_high(i, g):
                before(sc, s_bu, NG * i)
                sc.wait_ge(s_yf, NG * i + g + 1)
                sc.copy(y_h[:, :, P * g:P * g + P],
                        yf[:, g, :].rearrange("p (r t) -> p r t", r=PH)).then_inc(s_yh, 1)

            def scores_exp(i):
                sc.wait_ge(s_sm, 2 * (i + 1))
                sc.activation(coef_e[:, :], ps_c[0:CB, 0:E], ACT.Exp, bias=sc_st[:, 1:2],
                              scale=SCORE_SCALE, accum_out=sc_st[:, 2:3]).then_inc(s_se, 1)

            def z_high(j, g):
                before(sc, s_zt[g], 32 * j)
                sc.wait_ge(s_zf, NG * j + g + 1)
                sc.copy(z_h[:, :, P * g:P * g + P].rearrange("p r (b o) -> p r b o", b=BG),
                        zf[:, g, :].rearrange("p (b r o) -> p r b o", b=BG, r=PH)).then_inc(s_zh, 1)
                before(sc, s_xo[g], 16 * j)
                sc.wait_ge(s_xt, NG * j + g + 1)
                sc.copy(x1T[:, :, P * g:P * g + P].rearrange("p r (b o) -> p r b o", b=BG),
                        ps_b[g][:, :].rearrange("p (b o r) -> p r b o", b=BG, r=PH)).then_inc(s_xe, 1)

            def h_high(i, n):
                before(sc, s_bu, NG * i)
                sc.wait_ge(s_hf, NL * i + n + 1)
                sc.copy(h_h[:, TPB * n:TPB * n + TPB, :], hf[:, n, :, :]).then_inc(s_hh, 1)

            def gelu(j, k):
                sc.wait_ge(s_up, NB * j + k + 1)
                if k >= KR:
                    sc.wait_ge(s_dn, HT * j + (k - KR) * HPB // HPT + 1)
                sc.activation(act[:, k % KR, :], ps_up[k % 2][:, :], ACT.Gelu).then_inc(s_ga, 1)

            def out_tile(j, t):
                sc.wait_ge(s_dn, HT * j + t + 1)
                before(sc, s_so[t % 2], 16 * ((HT // 2) * j + t // 2))
                sc.copy(oT[:, t % 2, :], ps_dn[:, 0:TN]).then_inc(s_oe, 1)

            def heads(j):
                for t in range(HT):
                    for k in range(HPT // HPB):
                        gelu(j, t * (HPT // HPB) + k)
                    if t:
                        out_tile(j, t - 1)
                out_tile(j, HT - 1)

            def chunk(i):
                for g in range(NG):
                    y_high(i, g)
                scores_exp(i)
                for g in range(NG):
                    z_high(i - 1, g)
                for n in range(NL):
                    h_high(i, n)
                heads(i - 1)

            sc.dma_start(bk_sb[:, :], bk).then_inc(s_wk, 16)
            sc.dma_start(b2_sb[:, :], b2).then_inc(s_wk, 16)
            sc.dma_start(ig[:, :], idx_gather).then_inc(s_idx, 16)
            sc.dma_start(isc[:, :], idx_scatter).then_inc(s_idx, 16)
            sc.wait_ge(s_pa, 16)
            sc.wait_ge(s_cp, 1)
            sc.activation(h1[:, :], ps_c[:, 0:B], ACT.Gelu, bias=A("b0")).then_inc(s_cg, 1)
            sc.wait_ge(s_cp, 2)
            sc.activation(h2[:, :], ps_dn[:, 0:B], ACT.Gelu, bias=A("b1")).then_inc(s_cg, 1)
            sc.wait_ge(s_dv, 3)
            sc.activation(att[:, :], lg[:, :], ACT.Exp, bias=stat[:, 0:1],
                          accum_out=stat[:, 1:2]).then_inc(s_ce, 1)
            high(dw_h[:, :, :].rearrange("p r n -> p (r n)"), stage_w[:, 0, :], s_wd, 16)
            sc.wait_ge(s_bp, 1)
            for n, b in enumerate((*ps_up, ps_dn, ps_c)):
                last = sc.copy(mix_bias[:, BANK * n:BANK * n + BANK], b[:, :])
            last.then_inc(s_mb, 1)
            for g in range(NG):
                y_high(0, g)
            high(Wt_h[:, :, :].rearrange("p r n -> p (r n)"), stage_w[:, 1, :], s_ww, 16)
            scores_exp(0)
            high(up_h[:, :, :].rearrange("p r n -> p (r n)"), stage_w[:, 0, :], s_wu, 16)
            for n in range(NL):
                h_high(0, n)
            high(upf_s[:, :, :].rearrange("p h m -> p (h m)"), stage_w[:, 1, :], s_wf, 16 * HPT)
            chunk(1)
            with sc.Fori(2, NCH) as i:
                chunk(i)
            for g in range(NG):
                z_high(NCH - 1, g)
            heads(NCH - 1)

        @block.vector
        def _(ve):
            def low(dst, src, high_part, n):
                ve.wait_ge(s_hw, n)
                ve.tensor_tensor(dst, src, high_part.bitcast(F32), ALU.subtract).then_inc(s_lw, 1)

            def y_full(i, g):
                ve.wait_ge(s_mix, NG * i + g + 1)
                bias = mix_bias[:, bass.ds(i * TN + P * g, P)].unsqueeze(1).broadcast_to([P, PH, P])
                ve.tensor_tensor(yf[:, g, :].rearrange("p (r t) -> p r t", r=PH),
                                 ps_a[g][:, :].rearrange("p (r t) -> p r t", r=PH), bias,
                                 ALU.add).then_inc(s_yf, 1)
                ve.wait_ge(s_yf, NG * i + g + 1)
                ve.tensor_reduce(ysum[:, :, BG * g:BG * g + BG],
                                 yf[:, g, :].rearrange("p (r b o) -> p r b o", r=PH, b=BG),
                                 AX.X, ALU.add).then_inc(s_ys, 1)

            def y_low(i, g):
                ve.wait_ge(s_yh, NG * i + g + 1)
                cols = slice(P * g, P * g + P)
                ve.tensor_tensor(y_l[:, :, cols], yf[:, g, :].rearrange("p (r t) -> p r t", r=PH),
                                 y_h[:, :, cols].bitcast(F32), ALU.subtract).then_inc(s_yl, 1)

            def scores_softmax(i):
                ve.wait_ge(s_sc, i + 1)
                ve.reduce_max(sc_st[:, 0:1], ps_c[0:CB, 0:E], AX.X).then_inc(s_sm, 1)
                ve.wait_ge(s_sm, 2 * i + 1)
                ve.tensor_scalar(sc_st[:, 1:2], sc_st[:, 0:1], -SCORE_SCALE, None, ALU.mult).then_inc(s_sm, 1)
                ve.wait_ge(s_se, i + 1)
                ve.reciprocal(sc_st[:, 3:4], sc_st[:, 2:3]).then_inc(s_sr, 1)
                ve.wait_ge(s_sr, i + 1)
                ve.tensor_scalar(coef_b[:, :, :], coef_e[:, :].unsqueeze(2).broadcast_to([CB, E, R]),
                                 sc_st[:, 3:4], None, ALU.mult).then_inc(s_cf, 1)

            def coef_turned(i):
                ve.wait_ge(s_ct, i + 1)
                ve.tensor_copy(coefT[:, :, :],
                               ps_c[:, P:P + PH * CB].rearrange("p (t b) -> p t b", t=PH)).then_inc(s_cc, 1)

            def z_full(j, g):
                ve.wait_ge(s_cv, NG * j + g + 1)
                bias = conv_bias[:, bass.ds(j * TN + P * g, P)].rearrange("p (b o) -> p b o", b=BG)
                ve.tensor_tensor(zf[:, g, :].rearrange("p (b r o) -> p b r o", b=BG, r=PH),
                                 ps_a[g][:, :].rearrange("p (b r o) -> p b r o", b=BG, r=PH),
                                 bias.unsqueeze(2).broadcast_to([P, BG, PH, C]), ALU.add).then_inc(s_zf, 1)

            def z_low(j, g):
                before(ve, s_zt[g], 32 * j)
                ve.wait_ge(s_zh, NG * j + g + 1)
                ve.tensor_tensor(z_l[:, :, P * g:P * g + P].rearrange("p r (b o) -> p r b o", b=BG),
                                 zf[:, g, :].rearrange("p (b r o) -> p r b o", b=BG, r=PH),
                                 z_h[:, :, P * g:P * g + P].bitcast(F32).rearrange("p r (b o) -> p r b o", b=BG),
                                 ALU.subtract).then_inc(s_zl, 1)

            def h_full(i, n):
                ve.wait_ge(s_lo, NL * i + n + 1)
                ve.wait_ge(s_cc, i + 1)
                by = coefT[:, TPB * n:TPB * n + TPB, :].unsqueeze(3).broadcast_to([P, TPB, CB, C])
                ve.tensor_tensor(hf[:, n, :, :].rearrange("p t (b o) -> p t b o", b=CB),
                                 ps_a[n][:, :].rearrange("p (t b o) -> p t b o", t=TPB, b=CB), by,
                                 ALU.mult).then_inc(s_hf, 1)

            def h_low(i, n):
                ve.wait_ge(s_hh, NL * i + n + 1)
                ve.tensor_tensor(h_l[:, TPB * n:TPB * n + TPB, :], hf[:, n, :, :],
                                 h_h[:, TPB * n:TPB * n + TPB, :].bitcast(F32), ALU.subtract).then_inc(s_hl, 1)

            def x1_sum(i, g):
                ve.wait_ge(s_bu, NG * i + g + 1)
                before(ve, s_xp[g], 16 * BG * i)
                ve.tensor_tensor(x1[:, g, :], ps_b[g][:, :], xs[:, g, :], ALU.add).then_inc(s_x1, 1)

            def chunk(i):
                for g in range(NG):
                    y_full(i, g)
                for g in range(NG):
                    y_low(i, g)
                scores_softmax(i)
                z_full(i - 1, 0)
                z_low(i - 1, 0)
                coef_turned(i)
                z_full(i - 1, 1)
                z_low(i - 1, 1)
                for n in range(NL):
                    h_full(i, n)
                    h_low(i, n)
                for g in range(NG):
                    x1_sum(i, g)

            ve.memset(ones[:, :], 1.0).then_inc(s_one, 1)
            ve.wait_ge(s_cp, 3)
            ve.wait_ge(s_wk, 48)
            ve.tensor_tensor(lg[:, :], ps_c[0:B, P:P + NK], b2_sb[:, :], ALU.add).then_inc(s_dv, 1)
            ve.wait_ge(s_dv, 1)
            ve.reduce_max(stat[:, 2:3], lg[:, :], AX.X).then_inc(s_dv, 1)
            ve.wait_ge(s_dv, 2)
            ve.tensor_scalar(stat[:, 0:1], stat[:, 2:3], -1.0, None, ALU.mult).then_inc(s_dv, 1)
            ve.wait_ge(s_ce, 1)
            ve.reciprocal(stat[:, 3:4], stat[:, 1:2]).then_inc(s_dv, 1)
            ve.wait_ge(s_dv, 4)
            ve.tensor_scalar(lg[:, :], att[:, :], stat[:, 3:4], None, ALU.mult).then_inc(s_dv, 1)
            ve.wait_ge(s_cp, 4)
            ve.tensor_copy(attT[:, :], ps_dn[0:NK, P:P + B]).then_inc(s_dv, 1)
            ve.wait_ge(s_dv, 6)
            ve.tensor_tensor(stage_o[0:NK, :].rearrange("k (b o) -> k b o", b=B),
                             attT[:, :].unsqueeze(2).broadcast_to([NK, B, C]),
                             bk_sb[:, :].unsqueeze(1).broadcast_to([NK, B, C]), ALU.mult).then_inc(s_dv, 1)
            ve.wait_ge(s_mz, 1)
            ve.wait_ge(s_mk, 1)
            for q in range(BG):
                for n, b in enumerate((*ps_a, *ps_b)):
                    src = b[C * q:C * q + C, :].rearrange("p (o g q) -> p g o q", o=8, q=BG)[:, :, :, q]
                    last = ve.tensor_copy(mixer[C * q:C * q + C, :, C * q + 8 * n:C * q + 8 * n + 8], src)
            last.then_inc(s_mc, 1)
            ve.wait_ge(s_mb, 1)
            for g in range(NG):
                y_full(0, g)
            for g in range(NG):
                y_low(0, g)
            low(dw_l[:, :, :].rearrange("p r n -> p (r n)"), stage_w[:, 0, :],
                dw_h[:, :, :].rearrange("p r n -> p (r n)"), 1)
            ve.wait_ge(s_rp, 1)
            ve.tensor_copy(route[:, :, :], ps_b[0][:, 0:PH * E].rearrange("p (r e) -> p r e", r=PH)).then_inc(s_rt, 1)
            low(Wt_l[:, :, :].rearrange("p r n -> p (r n)"), stage_w[:, 1, :],
                Wt_h[:, :, :].rearrange("p r n -> p (r n)"), 2)
            scores_softmax(0)
            coef_turned(0)
            for n in range(NL):
                h_full(0, n)
                h_low(0, n)
            low(up_l[:, :, :].rearrange("p r n -> p (r n)"), stage_w[:, 0, :],
                up_h[:, :, :].rearrange("p r n -> p (r n)"), 3)
            ve.wait_ge(s_bp, 1)
            ve.wait_ge(s_pb, 16)
            ve.tensor_tensor(stage_o[:, :].rearrange("p (b o) -> p b o", b=B),
                             A("condT").unsqueeze(2).broadcast_to([P, B, C]),
                             Bp("cwT").unsqueeze(1).broadcast_to([P, B, C]), ALU.mult).then_inc(s_dv, 1)
            for g in range(NG):
                x1_sum(0, g)
            ve.wait_ge(s_bp, 2)
            for n, b in enumerate((*ps_up, ps_dn, ps_c)):
                last = ve.tensor_tensor(
                    conv_bias[:, BANK * n:BANK * n + BANK].rearrange("p (b o) -> p b o", o=C),
                    b[:, :].rearrange("p (b o) -> p b o", o=C),
                    Bp("side").unsqueeze(1).broadcast_to([P, BANK // C, C]), ALU.add)
            last.then_inc(s_cb, 1)
            low(upf_s[2 * DH:P, :, :].rearrange("p h m -> p (h m)"), stage_w[2 * DH:P, 1, :],
                upf_s[2 * DH:P, :, :].rearrange("p h m -> p (h m)"), 4)
            ve.wait_ge(s_cb, 1)
            chunk(1)
            with ve.Fori(2, NCH) as i:
                chunk(i)
            for g in range(NG):
                z_full(NCH - 1, g)
                z_low(NCH - 1, g)

        @block.tensor
        def _(pe):
            mm = pe.matmul

            def mix(i, g):
                pe.wait_ge(s_x[g], 16 * (i + 1))
                before(pe, s_hf, NL * (i - 1) + g + 1)
                for r in range(PH):
                    last = mm(ps_a[g][:, P * r:P * r + P], xs[:, g, P * r:P * r + P],
                              mixer[:, i * NG + g, :], start=True, stop=True)
                last.then_inc(s_mix, 1)

            def scores(i):
                pe.wait_ge(s_ys, NG * (i + 1))
                before(pe, s_cc, i)
                for r in range(PH):
                    last = mm(ps_c[0:CB, 0:E], ysum[:, r, :], route[:, r, :], start=r == 0, stop=r == PH - 1)
                last.then_inc(s_sc, 1)

            def turn_coef(i):
                pe.wait_ge(s_cf, i + 1)
                for t in range(PH):
                    last = mm(ps_c[:, P + CB * t:P + CB * t + CB], coef_b[:, 2 * t:2 * t + 2, :],
                              A("ident")[0:CB, 0:CB], start=True, stop=True)
                last.then_inc(s_ct, 1)

            def conv(j, g, last_chunk=False):
                pe.wait_ge(s_xp[g], 16 * BG * (j + 1))
                if last_chunk:
                    pe.wait_ge(s_hf, NL * j + g + 1)
                else:
                    pe.wait_ge(s_yf, NG * (j + 1) + g + 1)
                for b in range(BG):
                    for k in range(TAPB):
                        last = mm(ps_a[g][:, P * b:P * b + P], x1p[:, BG * g + b, k:k + M],
                                  Bp("W3")[:, P * k:P * k + P], start=k == 0, stop=k == TAPB - 1)
                last.then_inc(s_cv, 1)
                pe.wait_ge(s_x1, NG * j + g + 1)
                for b in range(BG):
                    last = pe.transpose(ps_b[g][:, P * b:P * b + P], x1p[:, BG * g + b, 1:1 + M], A("ident"))
                last.then_inc(s_xt, 1)

            def split_product(dst, lh, ll, rh, rl, start, stop):
                mm(dst, lh, rh, start=start, stop=False)
                mm(dst, lh, rl, start=False, stop=False)
                return mm(dst, ll, rh, start=False, stop=stop)

            def lora_down(i, n):
                if n == 0:
                    pe.wait_ge(s_yh, NG * (i + 1))
                    pe.wait_ge(s_yl, NG * (i + 1))
                if isinstance(i, int) and i == 0:
                    pe.wait_ge(s_yf, n + 1)
                else:
                    pe.wait_ge(s_zf, NG * (i - 1) + n + 1)
                for t in range(TPB):
                    w = slice(P * (TPB * n + t), P * (TPB * n + t) + P)
                    for r in range(PH):
                        last = split_product(ps_a[n][:, TN * t:TN * t + TN], dw_h[:, r, w], dw_l[:, r, w],
                                             y_h[:, r, :], y_l[:, r, :], r == 0, r == PH - 1)
                last.then_inc(s_lo, 1)

            def up_head(j, h):
                k = h // HPB
                pe.wait_ge(s_g[h % GR], 16 * ((H // GR) * j + h // GR + 1))
                if h % HPB == 0 and k >= 2:
                    pe.wait_ge(s_ga, NB * j + k - 1)
                at = TN * (h % HPB)
                last = mm(ps_up[k % 2][:, at:at + TN], upf_s[:, h, :], gat[:, h % GR, :], start=True, stop=True)
                if h % HPB == HPB - 1:
                    last.then_inc(s_up, 1)

            def down_heads(j, t):
                pe.wait_ge(s_ga, NB * j + (t + 1) * HPT // HPB)
                before(pe, s_oe, HT * j + t)
                for q in range(HPT):
                    h = HPT * t + q
                    at = TN * (h % HPB)
                    last = mm(ps_dn[DH * q:DH * q + DH, 0:TN], Bp("dn")[:, DH * h:DH * h + DH],
                              act[:, (h // HPB) % KR, at:at + TN], start=True, stop=True)
                last.then_inc(s_dn, 1)

            def base_up(i, g, j=None):
                if isinstance(i, int) and i == 0:
                    if g == 0:
                        pe.wait_ge(s_lw, 2)
                else:
                    pe.wait_ge(s_xe, NG * (i - 1) + g + 1)
                cols = slice(P * g, P * g + P)
                heads = iter(range(g * H // NG, (g + 1) * H // NG))
                for s in range(2 * PH):
                    r = s % PH
                    if s == PH and g == 0:
                        pe.wait_ge(s_hh, NL * (i + 1))
                        pe.wait_ge(s_hl, NL * (i + 1))
                        if isinstance(i, int) and i == 0:
                            pe.wait_ge(s_lw, 3)
                    src = (y_h, y_l, Wt_h, Wt_l) if s < PH else (h_h, h_l, up_h, up_l)
                    last = split_product(ps_b[g][:, :], src[0][:, r, cols], src[1][:, r, cols],
                                         src[2][:, r, :], src[3][:, r, :], s == 0, s == 2 * PH - 1)
                    if s == 2 * PH - 1:
                        last.then_inc(s_bu, 1)
                    if j is not None:
                        h = next(heads)
                        up_head(j, h)
                        if h % HPT == 1 and h // HPT > g * HT // NG:
                            down_heads(j, h // HPT - 1)
                if j is not None:
                    down_heads(j, (g + 1) * HT // NG - 1)

            def chunk(i):
                for g in range(NG):
                    mix(i, g)
                scores(i)
                conv(i - 1, 0)
                turn_coef(i)
                conv(i - 1, 1)
                for n in range(NL):
                    lora_down(i, n)
                for g in range(NG):
                    base_up(i, g, i - 1)

            pe.wait_ge(s_pa, 16)
            mm(ps_c[:, 0:B], A("W0"), A("condT"), start=True, stop=True).then_inc(s_cp, 1)
            pe.wait_ge(s_cg, 1)
            mm(ps_dn[:, 0:B], A("W1"), h1[:, :], start=True, stop=True).then_inc(s_cp, 1)
            pe.wait_ge(s_cg, 2)
            mm(ps_c[0:B, P:P + NK], h2[:, :], A("W2"), start=True, stop=True).then_inc(s_cp, 1)
            pe.wait_ge(s_dv, 5)
            pe.transpose(ps_dn[0:NK, P:P + B], lg[:, :], A("ident")[0:B, 0:B]).then_inc(s_cp, 1)
            pe.wait_ge(s_dv, 6)
            pe.wait_ge(s_wk, 48)
            for o in range(C):
                last = mm((*ps_a, *ps_b)[o // 8][:, B * (o % 8):B * (o % 8) + B], wK_sb[:, o, :], attT[:, :],
                          start=True, stop=True)
            last.then_inc(s_mk, 1)
            pe.wait_ge(s_dv, 7)
            pe.wait_ge(s_one, 1)
            for n, b in enumerate((*ps_up, ps_dn, ps_c)):
                last = mm(b[:, :], ones[0:NK, :], stage_o[0:NK, BANK * n:BANK * n + BANK], start=True, stop=True)
            last.then_inc(s_bp, 1)
            pe.wait_ge(s_mc, 1)
            for g in range(NG):
                mix(0, g)
            pe.wait_ge(s_pb, 16)
            for r in range(PH):
                last = mm(ps_b[0][:, E * r:E * r + E], Bp("Wq")[:, P * r:P * r + P], Bp("keysT"), start=True, stop=True)
            last.then_inc(s_rp, 1)
            pe.wait_ge(s_mb, 1)
            pe.wait_ge(s_rt, 1)
            scores(0)
            pe.wait_ge(s_lw, 1)
            lora_down(0, 0)
            turn_coef(0)
            lora_down(0, 1)
            for g in range(NG):
                base_up(0, g)
            pe.wait_ge(s_dv, 8)
            pe.wait_ge(s_cc, 1)
            for n, b in enumerate((*ps_up, ps_dn, ps_c)):
                last = mm(b[:, :], ones[:, :], stage_o[:, BANK * n:BANK * n + BANK], start=True, stop=True)
            last.then_inc(s_bp, 1)
            pe.wait_ge(s_cb, 1)
            pe.wait_ge(s_lw, 4)
            chunk(1)
            with pe.Fori(2, NCH) as i:
                chunk(i)
            for g in range(NG):
                conv(NCH - 1, g, last_chunk=True)
            for h in range(H):
                up_head(NCH - 1, h)
                if h % HPT == 1 and h > HPT:
                    down_heads(NCH - 1, h // HPT - 1)
            down_heads(NCH - 1, HT - 1)


def phased(a, axis):
    a = np.moveaxis(a, axis, -1)
    a = a.reshape(*a.shape[:-1], M, PH).swapaxes(-1, -2).reshape(*a.shape[:-1], L)
    return np.moveaxis(a, -1, axis)


def conv_blocks(w):
    out = np.zeros((C, PH, TAPB, PH, C), w.dtype)
    for o in range(C):
        rows = slice(o // CG * CG, o // CG * CG + CG)
        for rp in range(PH):
            for k in range(TAPB):
                for r in range(PH):
                    tap = PH * k + rp - r
                    if 0 <= tap < TAPS:
                        out[rows, rp, k, r, o] = w[o, :, tap]
    return out.reshape(P, TAPB * P)


def by_partition(a):
    return a.reshape(-1, P, a.shape[1]).swapaxes(0, 1).reshape(P, -1)


def kernel(**inputs):
    import concourse.bacc as bacc
    from concourse.bass_utils import run_bass_kernel_spmd

    a = {k: np.asarray(v) for k, v in inputs.items()}
    perm = a["L1_ffn_perm"]
    wk = a["L0_cond_weight"][..., 0].reshape(NK, C, 1, C)
    pack_a = [a["cond_128"].T, a["L0_cond_W0"], a["L0_cond_W1"], a["L0_cond_W2"], a["L0_cond_b0"][:, None],
              a["L0_cond_b1"][:, None], np.eye(P, dtype=np.float32)]
    pack_b = [a["L0_ffn_lora_keys"].T, a["L1_cond_c_weight"].T, np.tile(a["fside_S_0"], (P, 1)),
              phased(a["L0_ffn_Wq"], 1), conv_blocks(a["L1_cond_weight"]),
              a["L1_ffn_down"].transpose(1, 0, 2).reshape(MH, H * DH)]
    arrays = {
        "x": phased(a["x"].reshape(B * C, L), 1),
        "pack_a": np.concatenate(pack_a, 1),
        "pack_b": np.concatenate(pack_b, 1),
        "wK": np.tile(wk, (1, 1, BG, 1)).reshape(NK, C, P),
        "bk": a["L0_cond_bias_k"],
        "b2": np.tile(a["L0_cond_b2"], (B, 1)),
        "Wt": by_partition(phased(phased(a["L0_ffn_W_org"].T, 0), 1)),
        "down": by_partition(phased(a["L0_ffn_lora_down"].transpose(1, 0, 2).reshape(L, E * R), 0)),
        "up": by_partition(phased(a["L0_ffn_lora_up"].reshape(E * R, L), 1)),
        "upf": a["L1_ffn_up"].transpose(1, 0, 2).reshape(DH, H * MH),
        "idx_gather": np.tile(perm.reshape(H, DH).T, (HPT, 1)),
        "idx_scatter": perm.reshape(HT, P).T,
    }
    nc = bacc.Bacc("TRN2", target_bir_lowering=False, num_devices=1)
    feed, args = {}, []
    for name, v in arrays.items():
        v = feed[f"in_{name}"] = np.ascontiguousarray(v)
        args.append(nc.dram_tensor(f"in_{name}", v.shape, mybir.dt.from_np(v.dtype), kind="ExternalInput").ap())
    args.append(nc.dram_tensor("out_t", (L, B * C), F32, kind="ExternalOutput").ap())
    adaln_ffn(nc, *args)
    r = run_bass_kernel_spmd(nc, [feed], core_ids=[0])
    return np.ascontiguousarray(r.results[0]["out_t"].T.reshape(B, C, L))
```

```python
from contextlib import ExitStack

import numpy as np

import concourse.bass as bass
from concourse import mybir

ALU = mybir.AluOpType
ACT = mybir.ActivationFunctionType
AX = mybir.AxisListType
F32 = mybir.dt.float32
F32R = mybir.dt.float32r
I32 = mybir.dt.int32

P = 128
B, C, L = 64, 32, 512
E, R, KD = 8, 64, 128
NK = 8
H, DH, MH = 16, 32, 128
TAPS, CG = 9, 8
PH = 4
M = L // PH
BG = P // C
NG = 2
NCH = B // (BG * NG)
TN = P * NG
CB = BG * NG
BANK = 512
TPB = BANK // TN
NL = (E * R // P) // TPB
HPB = BANK // TN
NB = H // HPB
HT = H * DH // P
HPT = P // DH
GR = 8
KR = GR // HPB
EARLY = 3
SCORE_SCALE = 1.0 / (C * float(KD) ** 0.5)
assert NCH % 2 == 0 and NG == 2 and NL == 2
TAPB = 3

PACK_A = dict(condT=B, W0=P, W1=P, W2=NK, b0=1, b1=1, ident=P)
PACK_B = dict(keysT=E, cwT=C, side=C, Wq=L, W3=TAPB * P, dn=H * DH)


def offsets(pack):
    at, out = 0, {}
    for name, n in pack.items():
        out[name] = (at, at + n)
        at += n
    return out, at


def adaln_ffn(nc, x, pack_a, pack_b, wK, bk, b2, Wt, down, up, upf, idx_gather, idx_scatter, out):
    col_a, width_a = offsets(PACK_A)
    col_b, width_b = offsets(PACK_B)
    ctx = ExitStack()
    with ctx:
        def sb(name, shape, dt=F32):
            return ctx.enter_context(nc.sbuf_tensor(name, shape, dt))

        def sem(name):
            return ctx.enter_context(nc.semaphore(name))

        def bank(name):
            return ctx.enter_context(nc.psum_tensor(name, [P, BANK], F32))

        ps_a = [bank("ps_a0"), bank("ps_a1")]
        ps_b = [bank("ps_b0"), bank("ps_b1")]
        ps_up = [bank("ps_up0"), bank("ps_up1")]
        ps_dn = bank("ps_dn")
        ps_c = bank("ps_c")

        pa = sb("pa", [P, width_a])
        pb = sb("pb", [P, width_b])

        def A(name):
            return pa[:, col_a[name][0]:col_a[name][1]]

        def Bp(name):
            return pb[:, col_b[name][0]:col_b[name][1]]

        wK_sb = sb("wK_sb", [NK, C, P])
        bk_sb = sb("bk_sb", [NK, C])
        b2_sb = sb("b2_sb", [B, NK])
        ones = sb("ones", [P, P])
        stage_w = sb("stage_w", [P, 2, PH * L])
        stage_o = sb("stage_o", [P, B * C])
        Wt_h, Wt_l = sb("Wt_h", [P, PH, L], F32R), sb("Wt_l", [P, PH, L], F32R)
        dw_h, dw_l = sb("dw_h", [P, PH, L], F32R), sb("dw_l", [P, PH, L], F32R)
        up_h, up_l = sb("up_h", [P, PH, L], F32R), sb("up_l", [P, PH, L], F32R)
        upf_s = sb("upf_s", [P, H, MH], F32R)
        mixer = sb("mixer", [P, B // BG, P])
        mix_bias = sb("mix_bias", [P, B * C])
        conv_bias = sb("conv_bias", [P, B * C])
        route = sb("route", [P, PH, E])
        h1, h2 = sb("h1", [P, B]), sb("h2", [P, B])
        lg, att = sb("lg", [B, NK]), sb("att", [B, NK])
        attT = sb("attT", [NK, B])
        stat = sb("stat", [B, 4])
        ig = sb("ig", [P, H], I32)
        isc = sb("isc", [P, HT], I32)

        xs = sb("xs", [P, NG, L])
        xr = sb("xr", [P, NG, L])
        yf = sb("yf", [P, 2, L])
        y_h, y_l = sb("y_h", [P, PH, TN], F32R), sb("y_l", [P, PH, TN], F32R)
        ysum = sb("ysum", [P, PH, CB])
        sc_st = sb("sc_st", [CB, 4])
        coef_e = sb("coef_e", [CB, E])
        coef = sb("coef", [CB, E])
        coef_b = sb("coef_b", [CB, E, R])
        coefT = sb("coefT", [P, PH, CB])
        hf = sb("hf", [P, 2, TPB, TN])
        h_h, h_l = sb("h_h", [P, PH, TN], F32R), sb("h_l", [P, PH, TN], F32R)
        x1 = sb("x1", [P, NG, L])
        x1p = sb("x1p", [P, CB, M + 2])
        zf = sb("zf", [P, 2, BANK])
        z_h, z_l = sb("z_h", [P, PH, TN], F32R), sb("z_l", [P, PH, TN], F32R)
        x1T = sb("x1T", [P, PH, TN])
        gat = sb("gat", [P, GR, TN], F32R)
        act = sb("act", [P, KR, BANK])
        oT = sb("oT", [P, 2, TN])

        ztab = [nc.dram_tensor(f"ztab{n}", (2 * L, TN), F32, kind="Internal").ap() for n in range(2)]

        s_pa, s_pb, s_wk, s_idx = sem("pack_a_in"), sem("pack_b_in"), sem("kernels_in"), sem("index_in")
        s_wd, s_ww, s_wu, s_wf = sem("down_in"), sem("worg_in"), sem("up_in"), sem("heads_up_in")
        s_one = sem("ones_set")
        s_mz = sem("mixer_zeroed")
        s_pz = sem("pads_zeroed")
        s_cp = sem("cond_product")
        s_cg = sem("cond_gelu")
        s_dv = sem("vector_setup")
        s_ce = sem("cond_exp")
        s_mk = sem("mixer_product")
        s_mc = sem("mixer_copied")
        s_bp = sem("bias_product")
        s_mb = sem("mix_bias_set")
        s_cb = sem("conv_bias_set")
        s_rp, s_rt = sem("route_product"), sem("route_set")
        s_hw, s_lw = sem("weights_high"), sem("weights_low")
        s_x = [sem(f"x_in{g}") for g in range(NG)]
        s_xc = sem("x_kept")
        s_mix, s_yf, s_yh, s_yl, s_ys = sem("mixed"), sem("y_full"), sem("y_high"), sem("y_low"), sem("y_summed")
        s_sc, s_sm, s_se, s_sr = sem("scores"), sem("scores_max"), sem("scores_exp"), sem("scores_recip")
        s_cf, s_ct, s_cc = sem("coef_ready"), sem("coef_turned"), sem("coefT_copied")
        s_lo, s_hf, s_hh, s_hl = sem("lora_down"), sem("h_full"), sem("h_high"), sem("h_low")
        s_bu, s_x1 = sem("base_and_up"), sem("x1_ready")
        s_xp = [sem(f"x1_phases{g}") for g in range(NG)]
        s_cv, s_zf, s_zh, s_zl = sem("convolved"), sem("z_full"), sem("z_high"), sem("z_low")
        s_xt, s_xe = sem("x1_turned"), sem("x1T_copied")
        s_xo = [sem(f"x1T_out{g}") for g in range(NG)]
        s_zt = [sem(f"z_table{g}") for g in range(NG)]
        s_g = [sem(f"gathered{s}") for s in range(GR)]
        s_up, s_ga, s_dn, s_oe = sem("heads_up"), sem("activated"), sem("heads_down"), sem("oT_copied")
        s_so = [sem(f"scattered{s}") for s in range(2)]
        s_ix = sem("index_stepped")

        def before(eng, s, value):
            if not isinstance(value, int) or value > 0:
                eng.wait_ge(s, value)

        def there(j):
            return not isinstance(j, int) or 0 <= j < NCH

        block = ctx.enter_context(nc.Block())

        @block.sync
        def _(sp):
            def load_x(i, g):
                before(sp, s_mix, NG * (i - 1) + g + 1)
                before(sp, s_xc, NG * (i - 1) + g + 1)
                sp.dma_start(xs[:, g, :], x[bass.ds((i * NG + g) * P, P), :]).then_inc(s_x[g], 16)

            def phases(i, g):
                sp.wait_ge(s_x1, NG * i + g + 1)
                before(sp, s_xt, NG * (i - 1) + g + 1)
                for b in range(BG):
                    sp.dma_start(x1p[:, BG * g + b, 1:1 + M],
                                 x1[C * b:C * b + C, g, :].rearrange("c (r m) -> c r m", r=PH)).then_inc(s_xp[g], 16)

            def store_z(j, g, odd):
                if g == 0:
                    for s in range(GR):
                        before(sp, s_g[s], 16 * (H // GR) * (j - 1))
                cols = slice(P * g, P * g + P)
                sp.wait_ge(s_zh, NG * j + g + 1)
                sp.dma_start(ztab[odd][0:L, cols].rearrange("(m r) t -> m r t", r=PH),
                             z_h[:, :, cols].bitcast(F32)).then_inc(s_zt[g], 16)
                sp.wait_ge(s_zl, NG * j + g + 1)
                sp.dma_start(ztab[odd][L:2 * L, cols].rearrange("(m r) t -> m r t", r=PH),
                             z_l[:, :, cols].bitcast(F32)).then_inc(s_zt[g], 16)
                sp.wait_ge(s_xe, NG * j + g + 1)
                sp.dma_start(out[:, bass.ds(j * TN + P * g, P)].rearrange("(m r) t -> m r t", r=PH),
                             x1T[:, :, cols]).then_inc(s_xo[g], 16)

            def chunk(i, odd, more=True):
                for g in range(NG):
                    if there(i - 1):
                        store_z(i - 1, g, 1 - odd)
                    if more:
                        load_x(i + 1, g)
                for g in range(NG):
                    phases(i, g)

            sp.dma_start(pa[:, :], pack_a).then_inc(s_pa, 16)
            sp.dma_start(wK_sb[:, :, :], wK).then_inc(s_wk, 16)
            for g in range(NG):
                load_x(0, g)
            sp.dma_start(stage_w[:, 0, :], down).then_inc(s_wd, 16)
            sp.dma_start(stage_w[:, 1, :], Wt).then_inc(s_ww, 16)
            sp.dma_start(pb[:, :], pack_b).then_inc(s_pb, 16)
            sp.wait_ge(s_lw, 1)
            sp.dma_start(stage_w[:, 0, :], up).then_inc(s_wu, 16)
            sp.wait_ge(s_lw, 2)
            for q in range(HPT):
                sp.dma_start(stage_w[DH * q:DH * q + DH, 1, :], upf).then_inc(s_wf, 16)
            sp.wait_ge(s_pz, 1)
            for i in range(3):
                chunk(i, i % 2)
            with sp.Fori(3, NCH - 2, 2) as i:
                chunk(i, 1)
                chunk(i + 1, 0)
            chunk(NCH - 1, 1, more=False)
            for g in range(NG):
                store_z(NCH - 1, g, 1)
            for g in range(NG):
                sp.wait_ge(s_xo[g], 16 * NCH)
            for s in range(2):
                sp.wait_ge(s_so[s], 16 * (HT // 2) * NCH)

        @block.gpsimd
        def _(pool):
            limit = pool.alloc_register("limit")

            def value(v):
                if isinstance(v, int):
                    return v
                pool.reg_mov(limit, v)
                return limit

            def gather(j, h, odd):
                free = value(NB * j + (h - GR) // HPB + 1 if h >= GR else NB * (j - 1) + (h + H - GR) // HPB + 1)
                pool.wait_ge(s_ix, 3)
                before(pool, s_up, free)
                pool.indirect_dma_start(
                    out=gat[:, h % GR, :].bitcast(F32), out_offset=None, in_=ztab[odd],
                    in_offset=bass.IndirectOffsetOnAxis(ap=ig[:, h:h + 1], axis=0),
                ).then_inc(s_g[h % GR], 16)

            def scatter(j, t):
                ready = value(HT * j + t + 1)
                pool.wait_ge(s_ix, 3)
                pool.wait_ge(s_oe, ready)
                pool.indirect_dma_start(
                    out=out.rearrange("l (c t) -> (l c) t", t=TN),
                    out_offset=bass.IndirectOffsetOnAxis(ap=isc[:, t:t + 1], axis=0),
                    in_=oT[:, t % 2, :], in_offset=None, compute_op=ALU.add,
                ).then_inc(s_so[t % 2], 16)

            def chunk(j, odd):
                for g in range(NG):
                    pool.wait_ge(s_zt[g], 32 * (j + 1))
                for h in range(GR):
                    gather(j, h, odd)
                if not isinstance(j, int) or j > 0:
                    scatter(j - 1, HT - 1)
                for h in range(GR, GR + HPT):
                    gather(j, h, odd)
                if not isinstance(j, int) or j > 0:
                    done = value(16 * (HT // 2) * j)
                    pool.wait_ge(s_ix, 3)
                    for s in range(2):
                        pool.wait_ge(s_so[s], done)
                    pool.tensor_scalar(isc[:, :], isc[:, :], 1.0, None, ALU.add).then_inc(s_ix, 1)
                    pool.wait_ge(s_ix, j + 3)
                for g in range(NG):
                    pool.wait_ge(s_xo[g], 16 * (j + 1))
                scatter(j, 0)
                for h in range(GR + HPT, H):
                    gather(j, h, odd)
                for t in range(1, HT - 1):
                    scatter(j, t)

            pool.memset(mixer[:, :, :], 0.0).then_inc(s_mz, 1)
            pool.memset(x1p[:, :, :], 0.0).then_inc(s_pz, 1)
            pool.wait_ge(s_idx, 32)
            pool.wait_ge(s_mz, 1)
            pool.wait_ge(s_pz, 1)
            for n, q in enumerate((1, 3)):
                rows = slice(DH * q, DH * q + DH)
                pool.tensor_scalar(ig[rows, :], ig[rows, :], float(L), None, ALU.add).then_inc(s_ix, 1)
                pool.wait_ge(s_ix, n + 1)
            pool.tensor_scalar(isc[:, :], isc[:, :], float(NCH), None, ALU.mult).then_inc(s_ix, 1)
            pool.wait_ge(s_ix, 3)
            chunk(0, 0)
            with pool.Fori(1, NCH - 1, 2) as j:
                chunk(j, 1)
                chunk(j + 1, 0)
            chunk(NCH - 1, 1)
            scatter(NCH - 1, HT - 1)

        @block.scalar
        def _(sc):
            def high(dst, src, s, value):
                sc.wait_ge(s, value)
                sc.copy(dst, src).then_inc(s_hw, 1)

            def y_high(i, g):
                before(sc, s_bu, NG * i)
                sc.wait_ge(s_yf, NG * i + g + 1)
                sc.copy(y_h[:, :, P * g:P * g + P],
                        yf[:, g, :].rearrange("p (r t) -> p r t", r=PH)).then_inc(s_yh, 1)

            def scores_exp(i):
                sc.wait_ge(s_sm, 2 * (i + 1))
                sc.activation(coef_e[:, :], ps_c[0:CB, 0:E], ACT.Exp, bias=sc_st[:, 1:2],
                              scale=SCORE_SCALE, accum_out=sc_st[:, 2:3]).then_inc(s_se, 1)

            def z_high(j, g):
                before(sc, s_zt[g], 32 * j)
                sc.wait_ge(s_zf, NG * j + g + 1)
                sc.copy(z_h[:, :, P * g:P * g + P].rearrange("p r (b o) -> p r b o", b=BG),
                        zf[:, g, :].rearrange("p (b r o) -> p r b o", b=BG, r=PH)).then_inc(s_zh, 1)
                before(sc, s_xo[g], 16 * j)
                sc.wait_ge(s_xt, NG * j + g + 1)
                sc.copy(x1T[:, :, P * g:P * g + P].rearrange("p r (b o) -> p r b o", b=BG),
                        ps_b[g][:, :].rearrange("p (b o r) -> p r b o", b=BG, r=PH)).then_inc(s_xe, 1)

            def h_high(i, n):
                before(sc, s_bu, NG * i)
                sc.wait_ge(s_hf, NL * i + n + 1)
                sc.copy(h_h[:, TPB * n:TPB * n + TPB, :], hf[:, n, :, :]).then_inc(s_hh, 1)

            def gelu(j, k):
                sc.wait_ge(s_up, NB * j + k + 1)
                if k >= KR:
                    sc.wait_ge(s_dn, HT * j + (k - KR) * HPB // HPT + 1)
                sc.activation(act[:, k % KR, :], ps_up[k % 2][:, :], ACT.Gelu).then_inc(s_ga, 1)

            def out_tile(j, t):
                sc.wait_ge(s_dn, HT * j + t + 1)
                before(sc, s_so[t % 2], 16 * ((HT // 2) * j + t // 2))
                sc.copy(oT[:, t % 2, :], ps_dn[:, 0:TN]).then_inc(s_oe, 1)

            def keep_x(i, g):
                sc.wait_ge(s_x[g], 16 * (i + 1))
                before(sc, s_x1, NG * (i - 1) + g + 1)
                sc.copy(xr[:, g, :], xs[:, g, :]).then_inc(s_xc, 1)

            def late_heads(j, k):
                if there(j):
                    gelu(j, k)
                    if k % 2 == 0:
                        out_tile(j, k // 2 - 1)

            def early_heads(j):
                for k in range(EARLY):
                    gelu(j, k)
                out_tile(j, 0)

            def chunk(i):
                for g in range(NG):
                    y_high(i, g)
                scores_exp(i)
                z_high(i - 1, 0)
                late_heads(i - 2, 3)
                for g in range(NG):
                    keep_x(i, g)
                h_high(i, 0)
                late_heads(i - 2, 4)
                z_high(i - 1, 1)
                late_heads(i - 2, 5)
                h_high(i, 1)
                late_heads(i - 2, 6)
                late_heads(i - 2, 7)
                if there(i - 2):
                    out_tile(i - 2, HT - 1)
                early_heads(i - 1)

            sc.dma_start(bk_sb[:, :], bk).then_inc(s_wk, 16)
            sc.dma_start(b2_sb[:, :], b2).then_inc(s_wk, 16)
            sc.dma_start(ig[:, :], idx_gather).then_inc(s_idx, 16)
            sc.dma_start(isc[:, :], idx_scatter).then_inc(s_idx, 16)
            sc.wait_ge(s_pa, 16)
            sc.wait_ge(s_cp, 1)
            sc.activation(h1[:, :], ps_c[:, 0:B], ACT.Gelu, bias=A("b0")).then_inc(s_cg, 1)
            sc.wait_ge(s_cp, 2)
            sc.activation(h2[:, :], ps_dn[:, 0:B], ACT.Gelu, bias=A("b1")).then_inc(s_cg, 1)
            sc.wait_ge(s_dv, 3)
            sc.activation(att[:, :], lg[:, :], ACT.Exp, bias=stat[:, 0:1],
                          accum_out=stat[:, 1:2]).then_inc(s_ce, 1)
            high(dw_h[:, :, :].rearrange("p r n -> p (r n)"), stage_w[:, 0, :], s_wd, 16)
            sc.wait_ge(s_bp, 1)
            for n, b in enumerate((*ps_up, ps_dn, ps_c)):
                last = sc.copy(mix_bias[:, BANK * n:BANK * n + BANK], b[:, :])
            last.then_inc(s_mb, 1)
            for g in range(NG):
                y_high(0, g)
            for g in range(NG):
                keep_x(0, g)
            high(Wt_h[:, :, :].rearrange("p r n -> p (r n)"), stage_w[:, 1, :], s_ww, 16)
            scores_exp(0)
            high(up_h[:, :, :].rearrange("p r n -> p (r n)"), stage_w[:, 0, :], s_wu, 16)
            for n in range(NL):
                h_high(0, n)
            high(upf_s[:, :, :].rearrange("p h m -> p (h m)"), stage_w[:, 1, :], s_wf, 16 * HPT)
            for i in range(1, 3):
                chunk(i)
            with sc.Fori(3, NCH) as i:
                chunk(i)
            z_high(NCH - 1, 0)
            late_heads(NCH - 2, 3)
            late_heads(NCH - 2, 4)
            z_high(NCH - 1, 1)
            for k in range(5, NB):
                late_heads(NCH - 2, k)
            out_tile(NCH - 2, HT - 1)
            for k in range(NB):
                gelu(NCH - 1, k)
                if k and k % 2 == 0:
                    out_tile(NCH - 1, k // 2 - 1)
            out_tile(NCH - 1, HT - 1)

        @block.vector
        def _(ve):
            def low(dst, src, high_part, n):
                ve.wait_ge(s_hw, n)
                ve.tensor_tensor(dst, src, high_part.bitcast(F32), ALU.subtract).then_inc(s_lw, 1)

            def y_full(i, g):
                ve.wait_ge(s_mix, NG * i + g + 1)
                bias = mix_bias[:, bass.ds(i * TN + P * g, P)].unsqueeze(1).broadcast_to([P, PH, P])
                ve.tensor_tensor(yf[:, g, :].rearrange("p (r t) -> p r t", r=PH),
                                 ps_a[g][:, :].rearrange("p (r t) -> p r t", r=PH), bias,
                                 ALU.add).then_inc(s_yf, 1)
                ve.wait_ge(s_yf, NG * i + g + 1)
                ve.tensor_reduce(ysum[:, :, BG * g:BG * g + BG],
                                 yf[:, g, :].rearrange("p (r b o) -> p r b o", r=PH, b=BG),
                                 AX.X, ALU.add).then_inc(s_ys, 1)

            def y_low(i, g):
                ve.wait_ge(s_yh, NG * i + g + 1)
                cols = slice(P * g, P * g + P)
                ve.tensor_tensor(y_l[:, :, cols], yf[:, g, :].rearrange("p (r t) -> p r t", r=PH),
                                 y_h[:, :, cols].bitcast(F32), ALU.subtract).then_inc(s_yl, 1)

            def scores_softmax(i):
                ve.wait_ge(s_sc, i + 1)
                ve.reduce_max(sc_st[:, 0:1], ps_c[0:CB, 0:E], AX.X).then_inc(s_sm, 1)
                ve.wait_ge(s_sm, 2 * i + 1)
                ve.tensor_scalar(sc_st[:, 1:2], sc_st[:, 0:1], -SCORE_SCALE, None, ALU.mult).then_inc(s_sm, 1)
                ve.wait_ge(s_se, i + 1)
                ve.reciprocal(sc_st[:, 3:4], sc_st[:, 2:3]).then_inc(s_sr, 1)
                ve.wait_ge(s_sr, i + 1)
                ve.tensor_scalar(coef_b[:, :, :], coef_e[:, :].unsqueeze(2).broadcast_to([CB, E, R]),
                                 sc_st[:, 3:4], None, ALU.mult).then_inc(s_cf, 1)

            def coef_turned(i):
                ve.wait_ge(s_ct, i + 1)
                ve.tensor_copy(coefT[:, :, :],
                               ps_c[:, P:P + PH * CB].rearrange("p (t b) -> p t b", t=PH)).then_inc(s_cc, 1)

            def z_full(j, g):
                ve.wait_ge(s_cv, NG * j + g + 1)
                bias = conv_bias[:, bass.ds(j * TN + P * g, P)].rearrange("p (b o) -> p b o", b=BG)
                ve.tensor_tensor(zf[:, g, :].rearrange("p (b r o) -> p b r o", b=BG, r=PH),
                                 ps_a[0][:, :].rearrange("p (b r o) -> p b r o", b=BG, r=PH),
                                 bias.unsqueeze(2).broadcast_to([P, BG, PH, C]), ALU.add).then_inc(s_zf, 1)

            def z_low(j, g):
                before(ve, s_zt[g], 32 * j)
                ve.wait_ge(s_zh, NG * j + g + 1)
                ve.tensor_tensor(z_l[:, :, P * g:P * g + P].rearrange("p r (b o) -> p r b o", b=BG),
                                 zf[:, g, :].rearrange("p (b r o) -> p r b o", b=BG, r=PH),
                                 z_h[:, :, P * g:P * g + P].bitcast(F32).rearrange("p r (b o) -> p r b o", b=BG),
                                 ALU.subtract).then_inc(s_zl, 1)

            def h_full(i, n):
                ve.wait_ge(s_lo, NL * i + n + 1)
                ve.wait_ge(s_cc, i + 1)
                by = coefT[:, TPB * n:TPB * n + TPB, :].unsqueeze(3).broadcast_to([P, TPB, CB, C])
                ve.tensor_tensor(hf[:, n, :, :].rearrange("p t (b o) -> p t b o", b=CB),
                                 ps_a[1][:, :].rearrange("p (t b o) -> p t b o", t=TPB, b=CB), by,
                                 ALU.mult).then_inc(s_hf, 1)

            def h_low(i, n):
                ve.wait_ge(s_hh, NL * i + n + 1)
                ve.tensor_tensor(h_l[:, TPB * n:TPB * n + TPB, :], hf[:, n, :, :],
                                 h_h[:, TPB * n:TPB * n + TPB, :].bitcast(F32), ALU.subtract).then_inc(s_hl, 1)

            def x1_sum(i, g):
                ve.wait_ge(s_bu, NG * i + g + 1)
                before(ve, s_xp[g], 16 * BG * i)
                ve.wait_ge(s_xc, NG * i + g + 1)
                ve.tensor_tensor(x1[:, g, :], ps_b[g][:, :], xr[:, g, :], ALU.add).then_inc(s_x1, 1)

            def chunk(i, more=True):
                for g in range(NG):
                    y_low(i, g)
                scores_softmax(i)
                z_full(i - 1, 0)
                z_low(i - 1, 0)
                coef_turned(i)
                h_full(i, 0)
                h_low(i, 0)
                z_full(i - 1, 1)
                z_low(i - 1, 1)
                h_full(i, 1)
                h_low(i, 1)
                sums(i, more)

            def sums(i, more=True):
                x1_sum(i, 0)
                if more:
                    for g in range(NG):
                        y_full(i + 1, g)
                x1_sum(i, 1)

            ve.memset(ones[:, :], 1.0).then_inc(s_one, 1)
            ve.wait_ge(s_cp, 3)
            ve.wait_ge(s_wk, 48)
            ve.tensor_tensor(lg[:, :], ps_c[0:B, P:P + NK], b2_sb[:, :], ALU.add).then_inc(s_dv, 1)
            ve.wait_ge(s_dv, 1)
            ve.reduce_max(stat[:, 2:3], lg[:, :], AX.X).then_inc(s_dv, 1)
            ve.wait_ge(s_dv, 2)
            ve.tensor_scalar(stat[:, 0:1], stat[:, 2:3], -1.0, None, ALU.mult).then_inc(s_dv, 1)
            ve.wait_ge(s_ce, 1)
            ve.reciprocal(stat[:, 3:4], stat[:, 1:2]).then_inc(s_dv, 1)
            ve.wait_ge(s_dv, 4)
            ve.tensor_scalar(lg[:, :], att[:, :], stat[:, 3:4], None, ALU.mult).then_inc(s_dv, 1)
            ve.wait_ge(s_cp, 4)
            ve.tensor_copy(attT[:, :], ps_dn[0:NK, P:P + B]).then_inc(s_dv, 1)
            ve.wait_ge(s_dv, 6)
            ve.tensor_tensor(stage_o[0:NK, :].rearrange("k (b o) -> k b o", b=B),
                             attT[:, :].unsqueeze(2).broadcast_to([NK, B, C]),
                             bk_sb[:, :].unsqueeze(1).broadcast_to([NK, B, C]), ALU.mult).then_inc(s_dv, 1)
            ve.wait_ge(s_mz, 1)
            ve.wait_ge(s_mk, 1)
            for q in range(BG):
                for n, b in enumerate((*ps_a, *ps_b)):
                    src = b[C * q:C * q + C, :].rearrange("p (o g q) -> p g o q", o=8, q=BG)[:, :, :, q]
                    last = ve.tensor_copy(mixer[C * q:C * q + C, :, C * q + 8 * n:C * q + 8 * n + 8], src)
            last.then_inc(s_mc, 1)
            ve.wait_ge(s_mb, 1)
            for g in range(NG):
                y_full(0, g)
            for g in range(NG):
                y_low(0, g)
            low(dw_l[:, :, :].rearrange("p r n -> p (r n)"), stage_w[:, 0, :],
                dw_h[:, :, :].rearrange("p r n -> p (r n)"), 1)
            ve.wait_ge(s_rp, 1)
            ve.tensor_copy(route[:, :, :], ps_b[0][:, 0:PH * E].rearrange("p (r e) -> p r e", r=PH)).then_inc(s_rt, 1)
            low(Wt_l[:, :, :].rearrange("p r n -> p (r n)"), stage_w[:, 1, :],
                Wt_h[:, :, :].rearrange("p r n -> p (r n)"), 2)
            scores_softmax(0)
            coef_turned(0)
            for n in range(NL):
                h_full(0, n)
                h_low(0, n)
            low(up_l[:, :, :].rearrange("p r n -> p (r n)"), stage_w[:, 0, :],
                up_h[:, :, :].rearrange("p r n -> p (r n)"), 3)
            ve.wait_ge(s_bp, 1)
            ve.wait_ge(s_pb, 16)
            ve.tensor_tensor(stage_o[:, :].rearrange("p (b o) -> p b o", b=B),
                             A("condT").unsqueeze(2).broadcast_to([P, B, C]),
                             Bp("cwT").unsqueeze(1).broadcast_to([P, B, C]), ALU.mult).then_inc(s_dv, 1)
            sums(0)
            ve.wait_ge(s_bp, 2)
            for n, b in enumerate((*ps_up, ps_dn, ps_c)):
                last = ve.tensor_tensor(
                    conv_bias[:, BANK * n:BANK * n + BANK].rearrange("p (b o) -> p b o", o=C),
                    b[:, :].rearrange("p (b o) -> p b o", o=C),
                    Bp("side").unsqueeze(1).broadcast_to([P, BANK // C, C]), ALU.add)
            last.then_inc(s_cb, 1)
            low(upf_s[2 * DH:P, :, :].rearrange("p h m -> p (h m)"), stage_w[2 * DH:P, 1, :],
                upf_s[2 * DH:P, :, :].rearrange("p h m -> p (h m)"), 4)
            ve.wait_ge(s_cb, 1)
            chunk(1)
            with ve.Fori(2, NCH - 1) as i:
                chunk(i)
            chunk(NCH - 1, more=False)
            for g in range(NG):
                z_full(NCH - 1, g)
                z_low(NCH - 1, g)

        @block.tensor
        def _(pe):
            mm = pe.matmul

            def mix(i, g):
                pe.wait_ge(s_x[g], 16 * (i + 1))
                if g == 0:
                    before(pe, s_zf, NG * (i - 1))
                else:
                    before(pe, s_hf, NL * i)
                for r in range(PH):
                    last = mm(ps_a[g][:, P * r:P * r + P], xs[:, g, P * r:P * r + P],
                              mixer[:, i * NG + g, :], start=True, stop=True)
                last.then_inc(s_mix, 1)

            def scores(i):
                pe.wait_ge(s_ys, NG * (i + 1))
                before(pe, s_cc, i)
                for r in range(PH):
                    last = mm(ps_c[0:CB, 0:E], ysum[:, r, :], route[:, r, :], start=r == 0, stop=r == PH - 1)
                last.then_inc(s_sc, 1)

            def turn_coef(i):
                pe.wait_ge(s_cf, i + 1)
                for t in range(PH):
                    last = mm(ps_c[:, P + CB * t:P + CB * t + CB], coef_b[:, 2 * t:2 * t + 2, :],
                              A("ident")[0:CB, 0:CB], start=True, stop=True)
                last.then_inc(s_ct, 1)

            def conv(j, g, last_chunk=False):
                pe.wait_ge(s_xp[g], 16 * BG * (j + 1))
                if g == 0 and not last_chunk:
                    pe.wait_ge(s_yf, NG * (j + 1) + 1)
                else:
                    before(pe, s_zf, NG * j + g)
                for b in range(BG):
                    for k in range(TAPB):
                        last = mm(ps_a[0][:, P * b:P * b + P], x1p[:, BG * g + b, k:k + M],
                                  Bp("W3")[:, P * k:P * k + P], start=k == 0, stop=k == TAPB - 1)
                last.then_inc(s_cv, 1)
                pe.wait_ge(s_x1, NG * j + g + 1)
                for b in range(BG):
                    last = pe.transpose(ps_b[g][:, P * b:P * b + P], x1p[:, BG * g + b, 1:1 + M], A("ident"))
                last.then_inc(s_xt, 1)

            def split_product(dst, lh, ll, rh, rl, start, stop):
                mm(dst, lh, rh, start=start, stop=False)
                mm(dst, lh, rl, start=False, stop=False)
                return mm(dst, ll, rh, start=False, stop=stop)

            def lora_down(i, n):
                if n == 0:
                    pe.wait_ge(s_yh, NG * (i + 1))
                    pe.wait_ge(s_yl, NG * (i + 1))
                    pe.wait_ge(s_yf, NG * (i + 1))
                else:
                    pe.wait_ge(s_hf, NL * i + n)
                for t in range(TPB):
                    w = slice(P * (TPB * n + t), P * (TPB * n + t) + P)
                    for r in range(PH):
                        last = split_product(ps_a[1][:, TN * t:TN * t + TN], dw_h[:, r, w], dw_l[:, r, w],
                                             y_h[:, r, :], y_l[:, r, :], r == 0, r == PH - 1)
                last.then_inc(s_lo, 1)

            def up_head(j, h):
                k = h // HPB
                pe.wait_ge(s_g[h % GR], 16 * ((H // GR) * j + h // GR + 1))
                if h % HPB == 0 and k >= 2:
                    pe.wait_ge(s_ga, NB * j + k - 1)
                at = TN * (h % HPB)
                last = mm(ps_up[k % 2][:, at:at + TN], upf_s[:, h, :], gat[:, h % GR, :], start=True, stop=True)
                if h % HPB == HPB - 1:
                    last.then_inc(s_up, 1)

            def down_heads(j, t):
                pe.wait_ge(s_ga, NB * j + (t + 1) * HPT // HPB)
                before(pe, s_oe, HT * j + t)
                for q in range(HPT):
                    h = HPT * t + q
                    at = TN * (h % HPB)
                    last = mm(ps_dn[DH * q:DH * q + DH, 0:TN], Bp("dn")[:, DH * h:DH * h + DH],
                              act[:, (h // HPB) % KR, at:at + TN], start=True, stop=True)
                last.then_inc(s_dn, 1)

            def pair(j, k):
                if there(j):
                    for h in range(HPB * k, HPB * k + HPB):
                        up_head(j, h)

            def base_up(i, g, heads=()):
                if isinstance(i, int) and i == 0:
                    pe.wait_ge(s_lw, 2)
                else:
                    pe.wait_ge(s_xe, NG * (i - 1) + g + 1)
                cols = slice(P * g, P * g + P)
                for s in range(2 * PH):
                    r = s % PH
                    if s == PH and g == 0:
                        pe.wait_ge(s_hh, NL * (i + 1))
                        pe.wait_ge(s_hl, NL * (i + 1))
                        if isinstance(i, int) and i == 0:
                            pe.wait_ge(s_lw, 3)
                    src = (y_h, y_l, Wt_h, Wt_l) if s < PH else (h_h, h_l, up_h, up_l)
                    last = split_product(ps_b[g][:, :], src[0][:, r, cols], src[1][:, r, cols],
                                         src[2][:, r, :], src[3][:, r, :], s == 0, s == 2 * PH - 1)
                    if s == 2 * PH - 1:
                        last.then_inc(s_bu, 1)
                    for at, work, j, n in heads:
                        if at == s and there(j):
                            work(j, n)

            def down(j, t):
                if there(j):
                    down_heads(j, t)

            def chunk(i, more=True):
                scores(i)
                conv(i - 1, 0)
                pair(i - 2, 3)
                turn_coef(i)
                lora_down(i, 0)
                down(i - 2, 1)
                pair(i - 2, 4)
                conv(i - 1, 1)
                pair(i - 2, 5)
                lora_down(i, 1)
                down(i - 2, 2)
                pair(i - 2, 6)
                base_up(i, 0, [(1, pair, i - 2, 7), (4, down, i - 2, 3)])
                if more:
                    for g in range(NG):
                        mix(i + 1, g)
                base_up(i, 1, [(1, pair, i - 1, 0), (3, pair, i - 1, 1), (6, down, i - 1, 0), (7, pair, i - 1, 2)])

            pe.wait_ge(s_pa, 16)
            mm(ps_c[:, 0:B], A("W0"), A("condT"), start=True, stop=True).then_inc(s_cp, 1)
            pe.wait_ge(s_cg, 1)
            mm(ps_dn[:, 0:B], A("W1"), h1[:, :], start=True, stop=True).then_inc(s_cp, 1)
            pe.wait_ge(s_cg, 2)
            mm(ps_c[0:B, P:P + NK], h2[:, :], A("W2"), start=True, stop=True).then_inc(s_cp, 1)
            pe.wait_ge(s_dv, 5)
            pe.transpose(ps_dn[0:NK, P:P + B], lg[:, :], A("ident")[0:B, 0:B]).then_inc(s_cp, 1)
            pe.wait_ge(s_dv, 6)
            pe.wait_ge(s_wk, 48)
            for o in range(C):
                last = mm((*ps_a, *ps_b)[o // 8][:, B * (o % 8):B * (o % 8) + B], wK_sb[:, o, :], attT[:, :],
                          start=True, stop=True)
            last.then_inc(s_mk, 1)
            pe.wait_ge(s_dv, 7)
            pe.wait_ge(s_one, 1)
            for n, b in enumerate((*ps_up, ps_dn, ps_c)):
                last = mm(b[:, :], ones[0:NK, :], stage_o[0:NK, BANK * n:BANK * n + BANK], start=True, stop=True)
            last.then_inc(s_bp, 1)
            pe.wait_ge(s_mc, 1)
            for g in range(NG):
                mix(0, g)
            pe.wait_ge(s_pb, 16)
            for r in range(PH):
                last = mm(ps_b[0][:, E * r:E * r + E], Bp("Wq")[:, P * r:P * r + P], Bp("keysT"), start=True, stop=True)
            last.then_inc(s_rp, 1)
            pe.wait_ge(s_mb, 1)
            pe.wait_ge(s_rt, 1)
            scores(0)
            pe.wait_ge(s_lw, 1)
            lora_down(0, 0)
            turn_coef(0)
            lora_down(0, 1)
            base_up(0, 0)
            for g in range(NG):
                mix(1, g)
            base_up(0, 1)
            pe.wait_ge(s_dv, 8)
            pe.wait_ge(s_cc, 1)
            for n, b in enumerate((*ps_up, ps_dn, ps_c)):
                last = mm(b[:, :], ones[:, :], stage_o[:, BANK * n:BANK * n + BANK], start=True, stop=True)
            last.then_inc(s_bp, 1)
            pe.wait_ge(s_cb, 1)
            pe.wait_ge(s_lw, 4)
            chunk(1)
            with pe.Fori(2, NCH - 1) as i:
                chunk(i)
            chunk(NCH - 1, more=False)
            conv(NCH - 1, 0, last_chunk=True)
            pair(NCH - 2, 3)
            down(NCH - 2, 1)
            pair(NCH - 2, 4)
            conv(NCH - 1, 1, last_chunk=True)
            pair(NCH - 2, 5)
            down(NCH - 2, 2)
            pair(NCH - 2, 6)
            pair(NCH - 2, 7)
            down(NCH - 2, 3)
            for k in range(NB):
                pair(NCH - 1, k)
                if k and k % 2 == 0:
                    down(NCH - 1, k // 2 - 1)
            down(NCH - 1, HT - 1)


def phased(a, axis):
    a = np.moveaxis(a, axis, -1)
    a = a.reshape(*a.shape[:-1], M, PH).swapaxes(-1, -2).reshape(*a.shape[:-1], L)
    return np.moveaxis(a, -1, axis)


def conv_blocks(w):
    out = np.zeros((C, PH, TAPB, PH, C), w.dtype)
    for o in range(C):
        rows = slice(o // CG * CG, o // CG * CG + CG)
        for rp in range(PH):
            for k in range(TAPB):
                for r in range(PH):
                    tap = PH * k + rp - r
                    if 0 <= tap < TAPS:
                        out[rows, rp, k, r, o] = w[o, :, tap]
    return out.reshape(P, TAPB * P)


def by_partition(a):
    return a.reshape(-1, P, a.shape[1]).swapaxes(0, 1).reshape(P, -1)


def kernel(**inputs):
    import concourse.bacc as bacc
    from concourse.bass_utils import run_bass_kernel_spmd

    a = {k: np.asarray(v) for k, v in inputs.items()}
    perm = a["L1_ffn_perm"]
    wk = a["L0_cond_weight"][..., 0].reshape(NK, C, 1, C)
    pack_a = [a["cond_128"].T, a["L0_cond_W0"], a["L0_cond_W1"], a["L0_cond_W2"], a["L0_cond_b0"][:, None],
              a["L0_cond_b1"][:, None], np.eye(P, dtype=np.float32)]
    pack_b = [a["L0_ffn_lora_keys"].T, a["L1_cond_c_weight"].T, np.tile(a["fside_S_0"], (P, 1)),
              phased(a["L0_ffn_Wq"], 1), conv_blocks(a["L1_cond_weight"]),
              a["L1_ffn_down"].transpose(1, 0, 2).reshape(MH, H * DH)]
    arrays = {
        "x": phased(a["x"].reshape(B * C, L), 1),
        "pack_a": np.concatenate(pack_a, 1),
        "pack_b": np.concatenate(pack_b, 1),
        "wK": np.tile(wk, (1, 1, BG, 1)).reshape(NK, C, P),
        "bk": a["L0_cond_bias_k"],
        "b2": np.tile(a["L0_cond_b2"], (B, 1)),
        "Wt": by_partition(phased(phased(a["L0_ffn_W_org"].T, 0), 1)),
        "down": by_partition(phased(a["L0_ffn_lora_down"].transpose(1, 0, 2).reshape(L, E * R), 0)),
        "up": by_partition(phased(a["L0_ffn_lora_up"].reshape(E * R, L), 1)),
        "upf": a["L1_ffn_up"].transpose(1, 0, 2).reshape(DH, H * MH),
        "idx_gather": np.tile(perm.reshape(H, DH).T, (HPT, 1)),
        "idx_scatter": perm.reshape(HT, P).T,
    }
    nc = bacc.Bacc("TRN2", target_bir_lowering=False, num_devices=1)
    feed, args = {}, []
    for name, v in arrays.items():
        v = feed[f"in_{name}"] = np.ascontiguousarray(v)
        args.append(nc.dram_tensor(f"in_{name}", v.shape, mybir.dt.from_np(v.dtype), kind="ExternalInput").ap())
    args.append(nc.dram_tensor("out_t", (L, B * C), F32, kind="ExternalOutput").ap())
    adaln_ffn(nc, *args)
    r = run_bass_kernel_spmd(nc, [feed], core_ids=[0])
    return np.ascontiguousarray(r.results[0]["out_t"].T.reshape(B, C, L))
```

```python
from contextlib import ExitStack

import numpy as np

import concourse.bass as bass
from concourse import mybir

ALU = mybir.AluOpType
ACT = mybir.ActivationFunctionType
AX = mybir.AxisListType
F32 = mybir.dt.float32
F32R = mybir.dt.float32r
I32 = mybir.dt.int32

P = 128
B, C, L = 64, 32, 512
E, R, KD = 8, 64, 128
NK = 8
H, DH, MH = 16, 32, 128
TAPS, CG = 9, 8
PH = 4
M = L // PH
BG = P // C
NG = 2
NCH = B // (BG * NG)
TN = P * NG
CB = BG * NG
BANK = 512
TPB = BANK // TN
NL = (E * R // P) // TPB
HPB = BANK // TN
NB = H // HPB
HT = H * DH // P
HPT = P // DH
ND = HT // 2
GR = 16
KR = 6
EARLY = 3
WARM, WARM_LAST = 4, 3
SCORE_SCALE = 1.0 / (C * float(KD) ** 0.5)
assert NCH % 2 == 0 and NG == 2 and NL == 2
TAPB = 3

PACK_A = dict(condT=B, W0=P, b0=1, W1=P, W2=NK, b1=1, cwT=C, side=C, b2=NK, ident=P)
PACK_B = dict(keysT=E, Wq=L, W3=TAPB * P, dn=H * DH)


def offsets(pack):
    at, out = 0, {}
    for name, n in pack.items():
        out[name] = (at, at + n)
        at += n
    return out, at


def adaln_ffn(nc, x, pack_a, pack_b, wK, Wt, down, up, upf, idx, out):
    col_a, width_a = offsets(PACK_A)
    col_b, width_b = offsets(PACK_B)
    ctx = ExitStack()
    with ctx:
        def sb(name, shape, dt=F32):
            return ctx.enter_context(nc.sbuf_tensor(name, shape, dt))

        def sem(name):
            return ctx.enter_context(nc.semaphore(name))

        def bank(name):
            return ctx.enter_context(nc.psum_tensor(name, [P, BANK], F32))

        ps_a = [bank("ps_a0"), bank("ps_a1")]
        ps_b = [bank("ps_b0"), bank("ps_b1")]
        ps_up = [bank("ps_up0"), bank("ps_up1")]
        ps_dn = bank("ps_dn")
        ps_c = bank("ps_c")

        pa = sb("pa", [P, width_a])
        pb = sb("pb", [P, width_b])

        def A(name):
            return pa[:, col_a[name][0]:col_a[name][1]]

        def Bp(name):
            return pb[:, col_b[name][0]:col_b[name][1]]

        wK_sb = sb("wK_sb", [NK, C * C + C])
        ones = sb("ones", [CB, R])
        warm = sb("warm", [P, 2])
        stage_w = sb("stage_w", [P, 2, PH * L])
        Wt_h, Wt_l = sb("Wt_h", [P, PH, L], F32R), sb("Wt_l", [P, PH, L], F32R)
        dw_h, dw_l = sb("dw_h", [P, PH, L], F32R), sb("dw_l", [P, PH, L], F32R)
        up_h, up_l = sb("up_h", [P, PH, L], F32R), sb("up_l", [P, PH, L], F32R)
        upf_s = sb("upf_s", [P, H, MH], F32R)
        upf_x = sb("upf_x", [P, H // HPB, MH], F32R)
        mixer = sb("mixer", [P, B // BG, P])
        mix_bias = sb("mix_bias", [P, B * C])
        conv_bias = sb("conv_bias", [P, B * C])
        kern = sb("kern", [P, BANK])
        kern_b, ctx_b = sb("kern_b", [B, C]), sb("ctx_b", [B, C])
        route = sb("route", [P, PH, E])
        h1, h2 = sb("h1", [P, B]), sb("h2", [P, B])
        lg, att = sb("lg", [B, NK]), sb("att", [B, NK])
        attT = sb("attT", [NK, B])
        stat = sb("stat", [B, 4])
        index = sb("index", [P, H + H // HPB + HT], I32)
        ig = index[:, 0:H]
        ig_pair = index[:, H:H + H // HPB]
        isc = index[:, H + H // HPB:]
        isc_last = sb("isc_last", [P, HT], I32)

        xs = sb("xs", [P, NG, L])
        xr = sb("xr", [P, NG, L])
        yf = sb("yf", [P, 2, L])
        y_h, y_l = sb("y_h", [P, PH, TN], F32R), sb("y_l", [P, PH, TN], F32R)
        ysum = sb("ysum", [P, PH, CB])
        sc_st = sb("sc_st", [CB, 4])
        coef_e = sb("coef_e", [CB, E])
        coef = sb("coef", [CB, E])
        coef_d = sb("coef_d", [CB, P // R, PH, CB])
        coefT = sb("coefT", [P, PH, CB])
        hf = sb("hf", [P, 2, TPB, TN])
        h_h, h_l = sb("h_h", [P, PH, TN], F32R), sb("h_l", [P, PH, TN], F32R)
        x1 = sb("x1", [P, NG, L])
        x1p = sb("x1p", [P, CB, M + 2])
        zf = sb("zf", [P, 2, BANK])
        z_h, z_l = sb("z_h", [P, PH, TN], F32R), sb("z_l", [P, PH, TN], F32R)
        x1T = sb("x1T", [P, PH, TN])
        gat = sb("gat", [P, GR, TN], F32R)
        act = sb("act", [P, KR, BANK])
        stage_f = act[:, 0:H * MH // BANK, :].rearrange("p s t -> p (s t)")
        oT = sb("oT", [P, HT, TN])

        ztab = [nc.dram_tensor(f"ztab{n}", (2 * L, TN), F32, kind="Internal").ap() for n in range(2)]

        kern_tab = nc.dram_tensor("kern_tab", (B, C * C), F32, kind="Internal").ap()
        kern_b_tab = nc.dram_tensor("kern_b_tab", (1, B * C), F32, kind="Internal").ap()
        ctx_b_tab = nc.dram_tensor("ctx_b_tab", (1, B * C), F32, kind="Internal").ap()

        s_pa0, s_pa, s_pb = sem("first_layer_in"), sem("pack_a_in"), sem("pack_b_in")
        s_wk, s_idx = sem("kernels_in"), sem("index_in")
        s_wd, s_ww, s_wu, s_wf = sem("down_in"), sem("worg_in"), sem("up_in"), sem("heads_up_in")
        s_one = sem("constants_set")
        s_mz = sem("mixer_zeroed")
        s_pz = sem("pads_zeroed")
        s_cp = sem("cond_product")
        s_cg = sem("cond_gelu")
        s_dv = sem("vector_setup")
        s_ce = sem("cond_exp")
        s_kp = sem("kernel_products")
        s_kc, s_cc_b = sem("kernels_copied"), sem("context_added")
        s_kt, s_bt, s_ct_b = sem("kernels_stored"), sem("mix_bias_stored"), sem("conv_bias_stored")
        s_mx = [sem("mixers_in_first"), sem("mixers_in")]
        s_mb = [sem("mix_bias_in_first"), sem("mix_bias_in")]
        s_cb = sem("conv_bias_in")
        s_rp, s_rt = sem("route_product"), sem("route_set")
        s_hw, s_lw = sem("weights_high"), sem("weights_low")
        s_hx, s_lx = sem("pairs_high"), sem("pairs_low")
        s_x = [sem(f"x_in{g}") for g in range(NG)]
        s_xc = sem("x_kept")
        s_mix, s_yf, s_yh, s_yl, s_ys = sem("mixed"), sem("y_full"), sem("y_high"), sem("y_low"), sem("y_summed")
        s_yu = sem("y_multiplied")
        s_sc, s_sm, s_se, s_sr = sem("scores"), sem("scores_max"), sem("scores_exp"), sem("scores_recip")
        s_cn = sem("coef_normed")
        s_cf, s_ct, s_cc = sem("coef_ready"), sem("coef_turned"), sem("coefT_copied")
        s_lo, s_hf, s_hh, s_hl = sem("lora_down"), sem("h_full"), sem("h_high"), sem("h_low")
        s_bu, s_x1 = sem("base_and_up"), sem("x1_ready")
        s_xp = [sem(f"x1_phases{b}") for b in range(CB)]
        s_cv, s_zf, s_zh, s_zl = sem("convolved"), sem("z_full"), sem("z_high"), sem("z_low")
        s_xt, s_xe = sem("x1_turned"), sem("x1T_copied")
        s_xo = [sem(f"x1T_out{g}") for g in range(NG)]
        s_zt = [sem(f"z_table{g}") for g in range(NG)]
        s_g = [sem(f"gathered{s}") for s in range(GR)]
        s_up, s_ga, s_dn, s_oe = sem("heads_up"), sem("activated"), sem("heads_down"), sem("oT_copied")
        s_so = [sem(f"scattered{t}") for t in range(HT)]
        s_ix = sem("index_stepped")

        def before(eng, s, value):
            if not isinstance(value, int) or value > 0:
                eng.wait_ge(s, value)

        def pair_bank(k, q):
            return (ps_up, ps_b)[q][k % 2]

        def there(j):
            return not isinstance(j, int) or 0 <= j < NCH

        block = ctx.enter_context(nc.Block())

        @block.sync
        def _(sp):
            def load_x(i, g):
                before(sp, s_mix, NG * (i - 1) + g + 1)
                before(sp, s_xc, NG * (i - 1) + g + 1)
                sp.dma_start(xs[:, g, :], x[bass.ds((i * NG + g) * P, P), :]).then_inc(s_x[g], 16)

            def phases(i, g):
                sp.wait_ge(s_x1, NG * i + g + 1)
                before(sp, s_xt, NG * (i - 1) + g + 1)
                for b in range(BG):
                    sp.dma_start(x1p[:, BG * g + b, 1:1 + M],
                                 x1[C * b:C * b + C, g, :].rearrange("c (r m) -> c r m", r=PH)
                                 ).then_inc(s_xp[BG * g + b], 16)

            def store_z(j, g, odd):
                if g == 0:
                    for s in range(GR):
                        before(sp, s_g[s], 16 * (H // GR) * (j - 1))
                cols = slice(P * g, P * g + P)
                sp.wait_ge(s_zh, NG * j + g + 1)
                sp.dma_start(ztab[odd][0:L, cols].rearrange("(m r) t -> m r t", r=PH),
                             z_h[:, :, cols].bitcast(F32)).then_inc(s_zt[g], 16)
                sp.wait_ge(s_zl, NG * j + g + 1)
                sp.dma_start(ztab[odd][L:2 * L, cols].rearrange("(m r) t -> m r t", r=PH),
                             z_l[:, :, cols].bitcast(F32)).then_inc(s_zt[g], 16)
                sp.wait_ge(s_xe, NG * j + g + 1)
                sp.dma_start(out[:, bass.ds(j * TN + P * g, P)].rearrange("(m r) t -> m r t", r=PH),
                             x1T[:, :, cols]).then_inc(s_xo[g], 16)

            def chunk(i, odd, more=True):
                for g in range(NG):
                    if there(i - 1):
                        store_z(i - 1, g, 1 - odd)
                    if more:
                        load_x(i + 1, g)
                for g in range(NG):
                    phases(i, g)

            first = col_a["b0"][1]
            sp.dma_start(pa[:, 0:first], pack_a[:, 0:first]).then_inc(s_pa0, 16)
            sp.dma_start(pa[:, first:], pack_a[:, first:]).then_inc(s_pa, 16)
            sp.dma_start(wK_sb[:, :], wK).then_inc(s_wk, 16)
            sp.dma_start(index[:, :], idx).then_inc(s_idx, 16)
            for g in range(NG):
                load_x(0, g)
            sp.dma_start(stage_w[:, 0, :], down).then_inc(s_wd, 16)
            sp.dma_start(stage_w[:, 1, :], Wt).then_inc(s_ww, 16)
            sp.wait_ge(s_kc, 2)
            sp.dma_start(kern_tab.rearrange("b (h n) -> h b n", n=BANK), kern[:, :]).then_inc(s_kt, 16)
            sp.dma_start(kern_b_tab.rearrange("a (b o) -> (a b) o", b=B), kern_b[:, :]).then_inc(s_bt, 16)
            sp.dma_start(pb[:, :], pack_b).then_inc(s_pb, 16)
            sp.wait_ge(s_mz, 1)
            sp.wait_ge(s_kt, 16)
            for n in range(2):
                groups = slice(0, NG) if n == 0 else slice(NG, B // BG)
                cols = slice(P * groups.start, P * groups.stop)
                for q in range(BG):
                    sp.dma_start(mixer[C * q:C * q + C, groups, C * q:C * q + C],
                                 kern_tab.rearrange("(g q) (i o) -> q i g o", q=BG, i=C)[q, :, groups, :]
                                 ).then_inc(s_mx[n], 16)
                if n == 0:
                    sp.wait_ge(s_bt, 16)
                sp.dma_start(mix_bias[:, cols], kern_b_tab[:, cols].broadcast_to([P, cols.stop - cols.start])
                             ).then_inc(s_mb[n], 16)
                if n == 0:
                    sp.wait_ge(s_lw, 1)
                    sp.dma_start(stage_w[:, 0, :], up).then_inc(s_wu, 16)
            for q in range(HPT):
                sp.dma_start(stage_f[DH * q:DH * q + DH, :], upf).then_inc(s_wf, 16)
            sp.wait_ge(s_cc_b, 1)
            sp.dma_start(ctx_b_tab.rearrange("a (b o) -> (a b) o", b=B), ctx_b[:, :]).then_inc(s_ct_b, 16)
            sp.wait_ge(s_ct_b, 16)
            sp.dma_start(conv_bias[:, :], ctx_b_tab.broadcast_to([P, B * C])).then_inc(s_cb, 16)
            sp.wait_ge(s_pz, 1)
            for i in range(3):
                chunk(i, i % 2)
            with sp.Fori(3, NCH - 2, 2) as i:
                chunk(i, 1)
                chunk(i + 1, 0)
            chunk(NCH - 1, 1, more=False)
            for g in range(NG):
                store_z(NCH - 1, g, 1)
            for g in range(NG):
                sp.wait_ge(s_xo[g], 16 * NCH)
            for t in range(HT):
                sp.wait_ge(s_so[t], 16 * NCH)

        @block.gpsimd
        def _(pool):
            limit = pool.alloc_register("limit")
            SET = 4

            def value(v):
                if isinstance(v, int):
                    return v
                pool.reg_mov(limit, v)
                return limit

            def gather_pair(k):
                pool.wait_ge(s_ix, SET)
                pool.wait_ge(s_up, NB * (NCH - 2) + (H - GR + k) // HPB + 1)
                pool.indirect_dma_start(
                    out=gat[:, k, :].bitcast(F32), out_offset=None, in_=ztab[1],
                    in_offset=bass.IndirectOffsetOnAxis(ap=ig_pair[:, k:k + 1], axis=0),
                ).then_inc(s_g[k], 16)

            def gather(j, h, odd):
                free = value(NB * j + (h - GR) // HPB + 1 if h >= GR else NB * (j - 1) + (h + H - GR) // HPB + 1)
                pool.wait_ge(s_ix, SET)
                before(pool, s_up, free)
                pool.indirect_dma_start(
                    out=gat[:, h % GR, :].bitcast(F32), out_offset=None, in_=ztab[odd],
                    in_offset=bass.IndirectOffsetOnAxis(ap=ig[:, h:h + 1], axis=0),
                ).then_inc(s_g[h % GR], 16)

            def scatter(j, t, index=isc):
                ready = value(ND * (NCH - 1) + t + 1 if j is NCH - 1 else ND * j + t // 2 + 1)
                pool.wait_ge(s_ix, SET)
                pool.wait_ge(s_oe, ready)
                pool.indirect_dma_start(
                    out=out.rearrange("l (c t) -> (l c) t", t=TN),
                    out_offset=bass.IndirectOffsetOnAxis(ap=index[:, t:t + 1], axis=0),
                    in_=oT[:, t, :], in_offset=None, compute_op=ALU.add,
                ).then_inc(s_so[t], 16)

            def chunk(j, odd):
                for g in range(NG):
                    pool.wait_ge(s_zt[g], 32 * (j + 1))
                for h in range(H // 2):
                    gather(j, h, odd)
                if not isinstance(j, int) or j > 0:
                    for t in range(2, HT):
                        scatter(j - 1, t)
                for h in range(H // 2, H):
                    gather(j, h, odd)
                if not isinstance(j, int) or j > 0:
                    done = value(16 * j)
                    pool.wait_ge(s_ix, SET)
                    for t in range(HT):
                        pool.wait_ge(s_so[t], done)
                    pool.tensor_scalar(isc, isc, 1.0, None, ALU.add).then_inc(s_ix, 1)
                    pool.wait_ge(s_ix, j + SET)
                for g in range(NG):
                    pool.wait_ge(s_xo[g], 16 * (j + 1))
                for t in range(2):
                    scatter(j, t)

            pool.memset(mixer[:, :, :], 0.0).then_inc(s_mz, 1)
            pool.memset(x1p[:, :, :], 0.0).then_inc(s_pz, 1)
            pool.wait_ge(s_idx, 16)
            pool.wait_ge(s_mz, 1)
            pool.wait_ge(s_pz, 1)
            pool.tensor_scalar(isc_last[:, :], isc, float(NCH), float(NCH - 1), ALU.mult, ALU.add).then_inc(s_ix, 1)
            pool.wait_ge(s_ix, 1)
            pool.tensor_scalar(isc, isc, float(NCH), None, ALU.mult).then_inc(s_ix, 1)
            pool.wait_ge(s_ix, 2)
            for n, q in enumerate((1, 3)):
                rows = slice(DH * q, DH * q + DH)
                low_rows = index[rows, 0:H + H // HPB]
                pool.tensor_scalar(low_rows, low_rows, float(L), None, ALU.add).then_inc(s_ix, 1)
                pool.wait_ge(s_ix, n + 3)
            chunk(0, 0)
            with pool.Fori(1, NCH - 3, 2) as j:
                chunk(j, 1)
                chunk(j + 1, 0)
            chunk(NCH - 3, 1)
            chunk(NCH - 2, 0)
            for g in range(NG):
                pool.wait_ge(s_zt[g], 32 * NCH)
            for k in range(NB):
                gather_pair(k)
            for t in range(2, HT):
                scatter(NCH - 2, t)
            for g in range(NG):
                pool.wait_ge(s_xo[g], 16 * NCH)
            for t in range(HT):
                scatter(NCH - 1, t, isc_last)

        @block.scalar
        def _(sc):
            def high(dst, src, s, value):
                sc.wait_ge(s, value)
                sc.copy(dst, src).then_inc(s_hw, 1)

            def y_high(i, g):
                if g == 0:
                    before(sc, s_bu, NG * (i - 1) + 1)
                else:
                    before(sc, s_yu, i)
                sc.wait_ge(s_yf, NG * i + g + 1)
                sc.copy(y_h[:, :, P * g:P * g + P],
                        yf[:, g, :].rearrange("p (r t) -> p r t", r=PH)).then_inc(s_yh, 1)

            def scores_exp(i):
                sc.wait_ge(s_sm, 2 * (i + 1))
                sc.activation(coef_e[:, :], ps_c[0:CB, 0:E], ACT.Exp, bias=sc_st[:, 1:2],
                              scale=SCORE_SCALE, accum_out=sc_st[:, 2:3]).then_inc(s_se, 1)

            def z_high(j, g):
                before(sc, s_zt[g], 32 * j)
                sc.wait_ge(s_zf, NG * j + g + 1)
                sc.copy(z_h[:, :, P * g:P * g + P].rearrange("p r (b o) -> p r b o", b=BG),
                        zf[:, g, :].rearrange("p (b r o) -> p r b o", b=BG, r=PH)).then_inc(s_zh, 1)
                before(sc, s_xo[g], 16 * j)
                sc.wait_ge(s_xt, NG * j + g + 1)
                sc.copy(x1T[:, :, P * g:P * g + P].rearrange("p r (b o) -> p r b o", b=BG),
                        ps_b[g][:, :].rearrange("p (b o r) -> p r b o", b=BG, r=PH)).then_inc(s_xe, 1)

            def h_high(i, n):
                before(sc, s_bu, NG * i)
                sc.wait_ge(s_hf, NL * i + n + 1)
                sc.copy(h_h[:, TPB * n:TPB * n + TPB, :], hf[:, n, :, :]).then_inc(s_hh, 1)

            def gelu(j, k):
                if isinstance(j, int) and (j, k) == (0, 0):
                    sc.wait_ge(s_lw, 4)
                    sc.wait_ge(s_lx, 1)
                sc.wait_ge(s_up, NB * j + k + 1)
                if k >= KR:
                    sc.wait_ge(s_dn, ND * j + 1)
                sc.activation(act[:, k % KR, :], ps_up[k % 2][:, :], ACT.Gelu).then_inc(s_ga, 1)

            def out_tiles(j, d):
                sc.wait_ge(s_dn, ND * j + d + 1)
                for t in (2 * d, 2 * d + 1):
                    before(sc, s_so[t], 16 * j)
                sc.copy(oT[:, 2 * d:2 * d + 2, :].rearrange("p t n -> p (t n)"), ps_dn[:, :]).then_inc(s_oe, 1)

            def last_tile(t):
                sc.wait_ge(s_dn, ND * (NCH - 1) + t + 1)
                sc.wait_ge(s_so[t], 16 * (NCH - 1))
                sc.copy(oT[:, t, :], ps_dn[:, TN * (t % 2):TN * (t % 2) + TN]).then_inc(s_oe, 1)

            def keep_x(i, g):
                sc.wait_ge(s_x[g], 16 * (i + 1))
                before(sc, s_x1, NG * (i - 1) + g + 1)
                sc.copy(xr[:, g, :], xs[:, g, :]).then_inc(s_xc, 1)

            def late_heads(j, k):
                if there(j):
                    gelu(j, k)
                    if k == NB // 2:
                        out_tiles(j, 0)
                    if k == NB - 1:
                        out_tiles(j, 1)

            def next_y(i, j):
                for g in range(NG):
                    if there(i):
                        y_high(i, g)
                    if there(j):
                        gelu(j, g)
                if there(i):
                    scores_exp(i)
                if there(j):
                    for k in range(NG, EARLY):
                        gelu(j, k)

            def chunk(i):
                z_high(i - 1, 0)
                late_heads(i - 2, 3)
                for g in range(NG):
                    keep_x(i, g)
                h_high(i, 0)
                late_heads(i - 2, 4)
                z_high(i - 1, 1)
                late_heads(i - 2, 5)
                h_high(i, 1)
                late_heads(i - 2, 6)
                late_heads(i - 2, 7)
                next_y(i + 1, i - 1)

            sc.wait_ge(s_one, 1)
            sc.activation(warm[:, 1:2], warm[:, 0:1], ACT.Gelu)
            sc.wait_ge(s_pa0, 16)
            sc.wait_ge(s_cp, 1)
            sc.activation(h1[:, :], ps_c[:, 0:B], ACT.Gelu, bias=A("b0")).then_inc(s_cg, 1)
            sc.wait_ge(s_pa, 16)
            sc.wait_ge(s_cp, 2)
            sc.activation(h2[:, :], ps_dn[:, 0:B], ACT.Gelu, bias=A("b1")).then_inc(s_cg, 1)
            sc.wait_ge(s_dv, 3)
            sc.activation(att[:, :], lg[:, :], ACT.Exp, bias=stat[:, 0:1],
                          accum_out=stat[:, 1:2]).then_inc(s_ce, 1)
            high(dw_h[:, :, :].rearrange("p r n -> p (r n)"), stage_w[:, 0, :], s_wd, 16)
            high(Wt_h[:, :, :].rearrange("p r n -> p (r n)"), stage_w[:, 1, :], s_ww, 16)
            for g in range(NG):
                keep_x(0, g)
            for g in range(NG):
                y_high(0, g)
            scores_exp(0)
            high(up_h[:, :, :].rearrange("p r n -> p (r n)"), stage_w[:, 0, :], s_wu, 16)
            for n in range(NL):
                h_high(0, n)
            high(upf_s[:, :, :].rearrange("p h m -> p (h m)"), stage_f, s_wf, 16 * HPT)
            sc.copy(upf_x[2 * DH:P, :, :],
                    stage_f[2 * DH:P, :].rearrange("p (k h m) -> p k h m", h=HPB, m=MH)[:, :, 1, :]
                    ).then_inc(s_hx, 1)
            next_y(1, -1)
            for i in range(1, 3):
                chunk(i)
            with sc.Fori(3, NCH - 1) as i:
                chunk(i)
            chunk(NCH - 1)
            z_high(NCH - 1, 0)
            late_heads(NCH - 2, 3)
            z_high(NCH - 1, 1)
            for k in range(4, NB):
                late_heads(NCH - 2, k)
            for k in range(NB):
                if k >= KR:
                    sc.wait_ge(s_dn, ND * (NCH - 1) + (k - KR) * HPB // HPT + 1)
                for q in range(HPB):
                    sc.wait_ge(s_up, NB * (NCH - 1) + HPB * k + q + 1)
                    last = sc.activation(act[:, k % KR, TN * q:TN * q + TN], pair_bank(k, q)[:, 0:TN], ACT.Gelu)
                last.then_inc(s_ga, 1)
                if k and k % 2 == 0:
                    last_tile(k // 2 - 1)
            last_tile(HT - 1)

        @block.vector
        def _(ve):
            def low(dst, src, high_part, n):
                ve.wait_ge(s_hw, n)
                ve.tensor_tensor(dst, src, high_part.bitcast(F32), ALU.subtract).then_inc(s_lw, 1)

            def y_full(i, g):
                ve.wait_ge(s_mix, NG * i + g + 1)
                bias = mix_bias[:, bass.ds(i * TN + P * g, P)].unsqueeze(1).broadcast_to([P, PH, P])
                ve.tensor_tensor(yf[:, g, :].rearrange("p (r t) -> p r t", r=PH),
                                 ps_a[g][:, :].rearrange("p (r t) -> p r t", r=PH), bias,
                                 ALU.add).then_inc(s_yf, 1)
                ve.wait_ge(s_yf, NG * i + g + 1)
                ve.tensor_reduce(ysum[:, :, BG * g:BG * g + BG],
                                 yf[:, g, :].rearrange("p (r b o) -> p r b o", r=PH, b=BG),
                                 AX.X, ALU.add).then_inc(s_ys, 1)

            def y_low(i, g):
                ve.wait_ge(s_yh, NG * i + g + 1)
                cols = slice(P * g, P * g + P)
                ve.tensor_tensor(y_l[:, :, cols], yf[:, g, :].rearrange("p (r t) -> p r t", r=PH),
                                 y_h[:, :, cols].bitcast(F32), ALU.subtract).then_inc(s_yl, 1)

            def scores_softmax(i):
                ve.wait_ge(s_sc, i + 1)
                ve.reduce_max(sc_st[:, 0:1], ps_c[0:CB, 0:E], AX.X).then_inc(s_sm, 1)
                ve.wait_ge(s_sm, 2 * i + 1)
                ve.tensor_scalar(sc_st[:, 1:2], sc_st[:, 0:1], -SCORE_SCALE, None, ALU.mult).then_inc(s_sm, 1)
                ve.wait_ge(s_se, i + 1)
                ve.reciprocal(sc_st[:, 3:4], sc_st[:, 2:3]).then_inc(s_sr, 1)
                ve.wait_ge(s_sr, i + 1)
                ve.tensor_scalar(coef[:, :], coef_e[:, :], sc_st[:, 3:4], None, ALU.mult).then_inc(s_cn, 1)
                ve.wait_ge(s_cn, i + 1)
                ve.tensor_tensor(coef_d[:, :, :, :],
                                 coef[:, :].rearrange("b (t h) -> b h t", t=PH).unsqueeze(3).broadcast_to(
                                     [CB, P // R, PH, CB]),
                                 A("ident")[0:CB, 0:CB].unsqueeze(1).unsqueeze(1).broadcast_to([CB, P // R, PH, CB]),
                                 ALU.mult).then_inc(s_cf, 1)

            def coef_turned(i):
                ve.wait_ge(s_ct, i + 1)
                ve.tensor_copy(coefT[:, :, :],
                               ps_c[:, P:P + PH * CB].rearrange("p (t b) -> p t b", t=PH)).then_inc(s_cc, 1)

            def z_full(j, g, bank=ps_a[0]):
                ve.wait_ge(s_cv, NG * j + g + 1)
                bias = conv_bias[:, bass.ds(j * TN + P * g, P)].rearrange("p (b o) -> p b o", b=BG)
                ve.tensor_tensor(zf[:, g, :].rearrange("p (b r o) -> p b r o", b=BG, r=PH),
                                 bank[:, :].rearrange("p (b r o) -> p b r o", b=BG, r=PH),
                                 bias.unsqueeze(2).broadcast_to([P, BG, PH, C]), ALU.add).then_inc(s_zf, 1)

            def z_low(j, g):
                before(ve, s_zt[g], 32 * j)
                ve.wait_ge(s_zh, NG * j + g + 1)
                ve.tensor_tensor(z_l[:, :, P * g:P * g + P].rearrange("p r (b o) -> p r b o", b=BG),
                                 zf[:, g, :].rearrange("p (b r o) -> p r b o", b=BG, r=PH),
                                 z_h[:, :, P * g:P * g + P].bitcast(F32).rearrange("p r (b o) -> p r b o", b=BG),
                                 ALU.subtract).then_inc(s_zl, 1)

            def h_full(i, n, bank=ps_a[1]):
                ve.wait_ge(s_lo, NL * i + n + 1)
                ve.wait_ge(s_cc, i + 1)
                by = coefT[:, TPB * n:TPB * n + TPB, :].unsqueeze(3).broadcast_to([P, TPB, CB, C])
                ve.tensor_tensor(hf[:, n, :, :].rearrange("p t (b o) -> p t b o", b=CB),
                                 bank[:, :].rearrange("p (t b o) -> p t b o", t=TPB, b=CB), by,
                                 ALU.mult).then_inc(s_hf, 1)

            def h_low(i, n):
                ve.wait_ge(s_hh, NL * i + n + 1)
                ve.tensor_tensor(h_l[:, TPB * n:TPB * n + TPB, :], hf[:, n, :, :],
                                 h_h[:, TPB * n:TPB * n + TPB, :].bitcast(F32), ALU.subtract).then_inc(s_hl, 1)

            def x1_sum(i, g):
                ve.wait_ge(s_bu, NG * i + g + 1)
                for b in range(BG):
                    before(ve, s_xp[BG * g + b], 16 * i)
                ve.wait_ge(s_xc, NG * i + g + 1)
                ve.tensor_tensor(x1[:, g, :], ps_b[g][:, :], xr[:, g, :], ALU.add).then_inc(s_x1, 1)

            def chunk(i, more=True):
                z_full(i - 1, 0)
                z_low(i - 1, 0)
                coef_turned(i)
                h_full(i, 0)
                h_low(i, 0)
                z_full(i - 1, 1)
                z_low(i - 1, 1)
                h_full(i, 1)
                h_low(i, 1)
                sums(i, more)

            def sums(i, more=True):
                x1_sum(i, 0)
                if more:
                    for g in range(NG):
                        y_full(i + 1, g)
                    for g in range(NG):
                        y_low(i + 1, g)
                    scores_softmax(i + 1)
                x1_sum(i, 1)

            ve.memset(warm[:, :], 0.0).then_inc(s_one, 1)
            ve.memset(ones[:, :], 1.0).then_inc(s_one, 1)
            ve.wait_ge(s_cp, 3)
            ve.tensor_tensor(lg[:, :], ps_c[0:B, P:P + NK], A("b2")[0:B, :], ALU.add).then_inc(s_dv, 1)
            ve.wait_ge(s_dv, 1)
            ve.reduce_max(stat[:, 2:3], lg[:, :], AX.X).then_inc(s_dv, 1)
            ve.wait_ge(s_dv, 2)
            ve.tensor_scalar(stat[:, 0:1], stat[:, 2:3], -1.0, None, ALU.mult).then_inc(s_dv, 1)
            ve.wait_ge(s_ce, 1)
            ve.reciprocal(stat[:, 3:4], stat[:, 1:2]).then_inc(s_dv, 1)
            ve.wait_ge(s_dv, 4)
            ve.tensor_scalar(lg[:, :], att[:, :], stat[:, 3:4], None, ALU.mult).then_inc(s_dv, 1)
            ve.wait_ge(s_cp, 4)
            ve.tensor_copy(attT[:, :], ps_dn[0:NK, P:P + B]).then_inc(s_dv, 1)
            ve.wait_ge(s_kp, 1)
            ve.tensor_tensor(ctx_b[:, :], ps_up[1][0:B, 0:C], A("side")[0:B, :], ALU.add).then_inc(s_cc_b, 1)
            ve.wait_ge(s_kp, 2)
            ve.tensor_copy(kern_b[:, :], ps_up[0][0:B, 0:C]).then_inc(s_kc, 1)
            ve.wait_ge(s_kp, 3)
            ve.tensor_copy(kern[:, :], ps_b[0][:, :]).then_inc(s_kc, 1)
            low(dw_l[:, :, :].rearrange("p r n -> p (r n)"), stage_w[:, 0, :],
                dw_h[:, :, :].rearrange("p r n -> p (r n)"), 1)
            low(Wt_l[:, :, :].rearrange("p r n -> p (r n)"), stage_w[:, 1, :],
                Wt_h[:, :, :].rearrange("p r n -> p (r n)"), 2)
            ve.wait_ge(s_mb[0], 16)
            for g in range(NG):
                y_full(0, g)
                y_low(0, g)
            ve.wait_ge(s_rp, 1)
            ve.tensor_copy(route[:, :, :],
                           ps_up[0][:, P:P + PH * E].rearrange("p (r e) -> p r e", r=PH)).then_inc(s_rt, 1)
            scores_softmax(0)
            low(up_l[:, :, :].rearrange("p r n -> p (r n)"), stage_w[:, 0, :],
                up_h[:, :, :].rearrange("p r n -> p (r n)"), 3)
            coef_turned(0)
            for n in range(NL):
                h_full(0, n, ps_a[n])
                h_low(0, n)
            ve.wait_ge(s_mb[1], 16)
            sums(0)
            low(upf_s[2 * DH:P, :, :].rearrange("p h m -> p (h m)"), stage_f[2 * DH:P, :],
                upf_s[2 * DH:P, :, :].rearrange("p h m -> p (h m)"), 4)
            ve.tensor_tensor(upf_x[0:2 * DH, :, :],
                             stage_f[0:2 * DH, :].rearrange("p (k h m) -> p k h m", h=HPB, m=MH)[:, :, 0, :],
                             upf_s[0:2 * DH, :, :].rearrange("p (k h) m -> p k h m", h=HPB)[:, :, 0, :].bitcast(F32),
                             ALU.subtract).then_inc(s_lx, 1)
            ve.wait_ge(s_cb, 16)
            chunk(1)
            with ve.Fori(2, NCH - 1) as i:
                chunk(i)
            chunk(NCH - 1, more=False)
            for g in range(NG):
                z_full(NCH - 1, g, ps_a[g])
                z_low(NCH - 1, g)

        @block.tensor
        def _(pe):
            mm = pe.matmul

            def keep_clock(bank, n):
                for _ in range(n):
                    mm(bank[:, :], A("ident"), pa[:, 0:BANK], start=True, stop=True)

            def mix(i, g):
                pe.wait_ge(s_x[g], 16 * (i + 1))
                if g == 0:
                    before(pe, s_zf, NG * (i - 1))
                else:
                    before(pe, s_hf, NL * i)
                for r in range(PH):
                    last = mm(ps_a[g][:, P * r:P * r + P], xs[:, g, P * r:P * r + P],
                              mixer[:, i * NG + g, :], start=True, stop=True)
                last.then_inc(s_mix, 1)

            def scores(i):
                pe.wait_ge(s_ys, NG * (i + 1))
                before(pe, s_cc, i)
                for r in range(PH):
                    last = mm(ps_c[0:CB, 0:E], ysum[:, r, :], route[:, r, :], start=r == 0, stop=r == PH - 1)
                last.then_inc(s_sc, 1)

            def turn_coef(i):
                pe.wait_ge(s_cf, i + 1)
                for h in range(P // R):
                    last = mm(ps_c[R * h:R * h + R, P:P + PH * CB], ones[:, :],
                              coef_d[:, h, :, :].rearrange("k t b -> k (t b)"), start=True, stop=True)
                last.then_inc(s_ct, 1)

            def conv(j, g, last_chunk=False):
                bank = ps_a[g if last_chunk else 0]
                if g == 0 and not last_chunk:
                    pe.wait_ge(s_yf, NG * (j + 1) + 1)
                elif bank is ps_a[0]:
                    before(pe, s_zf, NG * j + g)
                else:
                    pe.wait_ge(s_hf, NL * (j + 1))
                for b in range(BG):
                    pe.wait_ge(s_xp[BG * g + b], 16 * (j + 1))
                    for k in range(TAPB):
                        last = mm(bank[:, P * b:P * b + P], x1p[:, BG * g + b, k:k + M],
                                  Bp("W3")[:, P * k:P * k + P], start=k == 0, stop=k == TAPB - 1)
                last.then_inc(s_cv, 1)
                pe.wait_ge(s_x1, NG * j + g + 1)
                for b in range(BG):
                    last = pe.transpose(ps_b[g][:, P * b:P * b + P], x1p[:, BG * g + b, 1:1 + M], A("ident"))
                last.then_inc(s_xt, 1)

            def split_product(dst, lh, ll, rh, rl, start, stop):
                mm(dst, lh, rh, start=start, stop=False)
                mm(dst, lh, rl, start=False, stop=False)
                return mm(dst, ll, rh, start=False, stop=stop)

            def lora_down(i, n, bank=ps_a[1]):
                if n == 0 or bank is ps_a[0]:
                    pe.wait_ge(s_yh, NG * (i + 1))
                    pe.wait_ge(s_yl, NG * (i + 1))
                    pe.wait_ge(s_yf, NG * (i + 1))
                elif there(i - 1):
                    pe.wait_ge(s_hf, NL * i + n)
                for t in range(TPB):
                    w = slice(P * (TPB * n + t), P * (TPB * n + t) + P)
                    for r in range(PH):
                        last = split_product(bank[:, TN * t:TN * t + TN], dw_h[:, r, w], dw_l[:, r, w],
                                             y_h[:, r, :], y_l[:, r, :], r == 0, r == PH - 1)
                last.then_inc(s_lo, 1)

            def up_head(j, h):
                k = h // HPB
                if isinstance(j, int) and (j, h) == (0, 0):
                    pe.wait_ge(s_lw, 4)
                pe.wait_ge(s_g[h % GR], 16 * ((H // GR) * j + h // GR + 1))
                if h % HPB == 0 and k >= 2:
                    pe.wait_ge(s_ga, NB * j + k - 1)
                at = TN * (h % HPB)
                last = mm(ps_up[k % 2][:, at:at + TN], upf_s[:, h, :], gat[:, h % GR, :], start=True, stop=True)
                if h % HPB == HPB - 1:
                    last.then_inc(s_up, 1)

            def up_pair(k):
                pe.wait_ge(s_g[k], 16 * ((H // GR) * (NCH - 1) + 1))
                pe.wait_ge(s_ga, NB * (NCH - 1) + k - 1)
                for q in range(HPB):
                    rows, bank = slice(2 * DH * q, 2 * DH * q + 2 * DH), pair_bank(k, q)
                    mm(bank[:, 0:TN], upf_s[rows, HPB * k + q, :], gat[rows, k, :], start=True, stop=False)
                    mm(bank[:, 0:TN], upf_x[rows, k, :], gat[rows, k, :], start=False, stop=True).then_inc(s_up, 1)

            def down_tile(t):
                for q in range(HPT):
                    h = HPT * t + q
                    at = TN * (h % HPB)
                    last = mm(ps_dn[DH * q:DH * q + DH, TN * (t % 2):TN * (t % 2) + TN],
                              Bp("dn")[:, DH * h:DH * h + DH], act[:, (h // HPB) % KR, at:at + TN],
                              start=True, stop=True)
                return last

            def down_heads(j, d):
                pe.wait_ge(s_ga, NB * j + (d + 1) * NB // ND)
                before(pe, s_oe, ND * j + d)
                for t in (2 * d, 2 * d + 1):
                    last = down_tile(t)
                last.then_inc(s_dn, 1)

            def down_last(t):
                pe.wait_ge(s_ga, NB * (NCH - 1) + (t + 1) * HPT // HPB)
                pe.wait_ge(s_oe, ND * (NCH - 1) + t)
                down_tile(t).then_inc(s_dn, 1)

            def pair(j, k):
                if there(j):
                    for h in range(HPB * k, HPB * k + HPB):
                        up_head(j, h)

            def base_up(i, g, others=(), steps=range(2 * PH)):
                first = isinstance(i, int) and i == 0
                cols = slice(P * g, P * g + P)
                for s in steps:
                    r = s % PH
                    if s == 0 and first:
                        pe.wait_ge(s_yh, g + 1)
                        pe.wait_ge(s_yl, g + 1)
                        pe.wait_ge(s_lw, 2)
                    elif s == 0:
                        pe.wait_ge(s_xe, NG * (i - 1) + g + 1)
                    if r % TPB == 0 and s >= PH and g == 0:
                        pe.wait_ge(s_hh, NL * i + r // TPB + 1)
                        pe.wait_ge(s_hl, NL * i + r // TPB + 1)
                        if first:
                            pe.wait_ge(s_lw, 3)
                    src = (y_h, y_l, Wt_h, Wt_l) if s < PH else (h_h, h_l, up_h, up_l)
                    last = split_product(ps_b[g][:, :], src[0][:, r, cols], src[1][:, r, cols],
                                         src[2][:, r, :], src[3][:, r, :], s == 0, s == 2 * PH - 1)
                    if s == 2 * PH - 1:
                        last.then_inc(s_bu, 1)
                    if s == PH - 1 and g == NG - 1:
                        last.then_inc(s_yu, 1)
                    for at, work, *which in others:
                        if at == s:
                            work(*which)

            def down(j, d):
                if there(j):
                    down_heads(j, d)

            def chunk(i, more=True):
                conv(i - 1, 0)
                pair(i - 2, 3)
                turn_coef(i)
                lora_down(i, 0)
                down(i - 2, 0)
                pair(i - 2, 4)
                conv(i - 1, 1)
                pair(i - 2, 5)
                lora_down(i, 1)
                pair(i - 2, 6)
                base_up(i, 0, [(1, pair, i - 2, 7), (4, down, i - 2, 1)])
                if more:
                    for g in range(NG):
                        mix(i + 1, g)
                after = [(1, pair, i - 1, 0), (3, pair, i - 1, 1), (6, pair, i - 1, 2)]
                if more:
                    after.append((4, scores, i + 1))
                base_up(i, 1, after)

            pe.wait_ge(s_pa0, 16)
            mm(ps_c[:, 0:B], A("W0"), A("condT"), start=True, stop=True).then_inc(s_cp, 1)
            pe.wait_ge(s_pa, 16)
            pe.wait_ge(s_cg, 1)
            mm(ps_dn[:, 0:B], A("W1"), h1[:, :], start=True, stop=True).then_inc(s_cp, 1)
            pe.wait_ge(s_cg, 2)
            mm(ps_c[0:B, P:P + NK], h2[:, :], A("W2"), start=True, stop=True).then_inc(s_cp, 1)
            pe.wait_ge(s_dv, 5)
            pe.transpose(ps_dn[0:NK, P:P + B], lg[:, :], A("ident")[0:B, 0:B]).then_inc(s_cp, 1)
            mm(ps_up[1][0:B, 0:C], A("condT"), A("cwT"), start=True, stop=True).then_inc(s_kp, 1)
            pe.wait_ge(s_dv, 6)
            pe.wait_ge(s_wk, 16)
            mm(ps_up[0][0:B, 0:C], attT[:, :], wK_sb[:, C * C:C * C + C], start=True, stop=True).then_inc(s_kp, 1)
            for n in range(C * C // BANK):
                last = mm(ps_b[0][B * n:B * n + B, :], attT[:, :], wK_sb[:, BANK * n:BANK * n + BANK],
                          start=True, stop=True)
            last.then_inc(s_kp, 1)
            keep_clock(ps_dn, WARM)
            pe.wait_ge(s_mx[0], 16 * BG)
            for g in range(NG):
                mix(0, g)
            pe.wait_ge(s_pb, 16)
            pe.wait_ge(s_kc, 1)
            for r in range(PH):
                last = mm(ps_up[0][:, P + E * r:P + E * r + E], Bp("Wq")[:, P * r:P * r + P], Bp("keysT"),
                          start=True, stop=True)
            last.then_inc(s_rp, 1)
            base_up(0, 0, steps=range(PH))
            pe.wait_ge(s_rt, 1)
            scores(0)
            pe.wait_ge(s_one, 2)
            pe.wait_ge(s_lw, 1)
            lora_down(0, 0, ps_a[0])
            turn_coef(0)
            lora_down(0, 1, ps_a[1])
            base_up(0, 1, steps=range(PH))
            base_up(0, 0, steps=range(PH, 2 * PH))
            pe.wait_ge(s_mx[1], 16 * BG)
            for g in range(NG):
                mix(1, g)
            base_up(0, 1, [(2 * PH - 1, scores, 1)], range(PH, 2 * PH))
            chunk(1)
            with pe.Fori(2, NCH - 1) as i:
                chunk(i)
            chunk(NCH - 1, more=False)
            conv(NCH - 1, 0, last_chunk=True)
            pair(NCH - 2, 3)
            conv(NCH - 1, 1, last_chunk=True)
            down(NCH - 2, 0)
            for k in range(NB // 2, NB):
                pair(NCH - 2, k)
            down(NCH - 2, 1)
            pe.wait_ge(s_cc, NCH)
            keep_clock(ps_c, WARM_LAST)
            pe.wait_ge(s_hx, 1)
            pe.wait_ge(s_lx, 1)
            pe.wait_ge(s_xe, NG * NCH)
            for k in range(NB):
                up_pair(k)
                if k and k % 2 == 0:
                    down_last(k // 2 - 1)
            down_last(HT - 1)


def phased(a, axis):
    a = np.moveaxis(a, axis, -1)
    a = a.reshape(*a.shape[:-1], M, PH).swapaxes(-1, -2).reshape(*a.shape[:-1], L)
    return np.moveaxis(a, -1, axis)


def conv_blocks(w):
    out = np.zeros((C, PH, TAPB, PH, C), w.dtype)
    for o in range(C):
        rows = slice(o // CG * CG, o // CG * CG + CG)
        for rp in range(PH):
            for k in range(TAPB):
                for r in range(PH):
                    tap = PH * k + rp - r
                    if 0 <= tap < TAPS:
                        out[rows, rp, k, r, o] = w[o, :, tap]
    return out.reshape(P, TAPB * P)


def by_partition(a):
    return a.reshape(-1, P, a.shape[1]).swapaxes(0, 1).reshape(P, -1)


def kernel(**inputs):
    import concourse.bacc as bacc
    from concourse.bass_utils import run_bass_kernel_spmd

    a = {k: np.asarray(v) for k, v in inputs.items()}
    perm = a["L1_ffn_perm"]
    pack_a = [a["cond_128"].T, a["L0_cond_W0"], a["L0_cond_b0"][:, None], a["L0_cond_W1"], a["L0_cond_W2"],
              a["L0_cond_b1"][:, None], a["L1_cond_c_weight"].T, np.tile(a["fside_S_0"], (P, 1)),
              np.tile(a["L0_cond_b2"], (P, 1)), np.eye(P, dtype=np.float32)]
    pack_b = [a["L0_ffn_lora_keys"].T, phased(a["L0_ffn_Wq"], 1), conv_blocks(a["L1_cond_weight"]),
              a["L1_ffn_down"].transpose(1, 0, 2).reshape(MH, H * DH)]
    arrays = {
        "x": phased(a["x"].reshape(B * C, L), 1),
        "pack_a": np.concatenate(pack_a, 1),
        "pack_b": np.concatenate(pack_b, 1),
        "wK": np.concatenate([a["L0_cond_weight"][..., 0].swapaxes(1, 2).reshape(NK, C * C),
                              a["L0_cond_bias_k"]], 1),
        "Wt": by_partition(phased(phased(a["L0_ffn_W_org"].T, 0), 1)),
        "down": by_partition(phased(a["L0_ffn_lora_down"].transpose(1, 0, 2).reshape(L, E * R), 0)),
        "up": by_partition(phased(a["L0_ffn_lora_up"].reshape(E * R, L), 1)),
        "upf": a["L1_ffn_up"].transpose(1, 0, 2).reshape(DH, H * MH),
        "idx": np.concatenate([
            np.tile(perm.reshape(H, DH).T, (HPT, 1)),
            np.repeat(perm.reshape(H // HPB, HPB, 1, DH), 2, 2).reshape(H // HPB, P).T, perm.reshape(HT, P).T], 1),
    }
    nc = bacc.Bacc("TRN2", target_bir_lowering=False, num_devices=1)
    feed, args = {}, []
    for name, v in arrays.items():
        v = feed[f"in_{name}"] = np.ascontiguousarray(v)
        args.append(nc.dram_tensor(f"in_{name}", v.shape, mybir.dt.from_np(v.dtype), kind="ExternalInput").ap())
    args.append(nc.dram_tensor("out_t", (L, B * C), F32, kind="ExternalOutput").ap())
    adaln_ffn(nc, *args)
    r = run_bass_kernel_spmd(nc, [feed], core_ids=[0])
    return np.ascontiguousarray(r.results[0]["out_t"].T.reshape(B, C, L))
```
